# Optimizing a Trainium2 kernel written in Bass

```python
import numpy as np
import jax
import jax.numpy as jnp

def _softmax(x, axis=-1):
    return jax.nn.softmax(x, axis=axis)

def _gelu(x):
    return jax.nn.gelu(x, approximate=True)

def _silu(x):
    return jax.nn.silu(x)

def _sigmoid(x):
    return jax.nn.sigmoid(x)

def _layernorm(x, axis=-1, eps=1e-05):
    m = jnp.mean(x, axis=axis, keepdims=True)
    v = jnp.var(x, axis=axis, keepdims=True)
    return (x - m) / jnp.sqrt(v + eps)

def _scatter_add(tgt, idx, src, axis=0):
    return tgt.at[idx].add(src)

def _segment_sum(src, seg, n):
    return jax.ops.segment_sum(src, seg, n)
kernel_name = 'mk_pixart_seq_d4_seqx_r8_6cc8f3'

def setup_inputs(seed: int=0):
    np.random.seed(seed)
    _w = jnp.asarray

    def _rec_inputs():
        import jax
        import jax.numpy as jnp
        _rk = jax.random.key(seed)
        x = -0.0002928 + 1 * jax.random.normal(jax.random.fold_in(_rk, 1), (32, 100, 128), jnp.float32)
        _lenS = 100 - jax.random.randint(jax.random.fold_in(_rk, 7), (32,), 0, max(1, 100 // 4) + 1, jnp.int32)
        _lenS2 = 1444 - jax.random.randint(jax.random.fold_in(_rk, 8), (32,), 0, max(1, 1444 // 4) + 1, jnp.int32)
        cond_1024 = 0.0061147 + 1.02565 * jax.random.normal(jax.random.fold_in(_rk, 11), (32, 128), jnp.float32)
        _ctx_1024P = jax.random.normal(jax.random.fold_in(_rk, 12), (32, 16, 128), jnp.float32)
        _ctx_1024c = jax.random.dirichlet(jax.random.fold_in(_rk, 512), 0.3 * jnp.ones((16,), jnp.float32), (32, 1444))
        _ctx_1024t = jnp.einsum('bsk,bkd->bsd', _ctx_1024c, _ctx_1024P)
        _ctx_1024t = _ctx_1024t * jax.lax.rsqrt(jnp.mean(jnp.square(_ctx_1024t)) + 1e-12) * 0.953939
        ctx_1024 = -0.00265004 + 0.998804 * (_ctx_1024t + 0.3 * jax.random.normal(jax.random.fold_in(_rk, 612), (32, 1444, 128), jnp.float32))
        return (x, cond_1024, ctx_1024)
    x, cond_1024, ctx_1024 = _rec_inputs()

    def _L0_xcond_setup():
        import jax, jax.numpy as jnp
        import numpy as np
        LN_EPS = 1e-06

        def _ln(x):
            mu = jnp.mean(x, axis=-1, keepdims=True)
            var = jnp.var(x, axis=-1, keepdims=True)
            return (x - mu) * jax.lax.rsqrt(var + LN_EPS)
        key = jax.random.key(seed)
        H, NH = (128, 16)
        B, N, S = (4, 128, 77)
        MLP = int(H * 4.0)
        ks = jax.random.split(key, 20)
        s = 1.0 / np.sqrt(H)
        return {'x': jax.random.normal(ks[0], (B, N, H), jnp.float32), 'c': jax.random.normal(ks[1], (B, H), jnp.float32), 'context': jax.random.normal(ks[2], (B, S, H), jnp.float32), 'W_mod': jax.random.normal(ks[3], (H, 6 * H), jnp.float32) * s, 'b_mod': jnp.zeros((6 * H,), jnp.float32), 'W_qkv': jax.random.normal(ks[4], (H, 3 * H), jnp.float32) * s, 'b_qkv': jnp.zeros((3 * H,), jnp.float32), 'W_proj': jax.random.normal(ks[5], (H, H), jnp.float32) * s, 'b_proj': jnp.zeros((H,), jnp.float32), 'W_qc': jax.random.normal(ks[6], (H, H), jnp.float32) * s, 'b_qc': jnp.zeros((H,), jnp.float32), 'W_kvc': jax.random.normal(ks[7], (H, 2 * H), jnp.float32) * s, 'b_kvc': jnp.zeros((2 * H,), jnp.float32), 'W_cproj': jax.random.normal(ks[8], (H, H), jnp.float32) * s, 'b_cproj': jnp.zeros((H,), jnp.float32), 'W_mlp1': jax.random.normal(ks[9], (H, MLP), jnp.float32) * s, 'b_mlp1': jnp.zeros((MLP,), jnp.float32), 'W_mlp2': jax.random.normal(ks[10], (MLP, H), jnp.float32) * (1.0 / np.sqrt(MLP)), 'b_mlp2': jnp.zeros((H,), jnp.float32)}
    _L0_xcond_all = _L0_xcond_setup()
    _L0_xcond_in = {k: v for k, v in _L0_xcond_all.items() if k in ('W_mod', 'b_mod', 'W_qkv', 'b_qkv', 'W_proj', 'b_proj', 'W_qc', 'b_qc', 'W_kvc', 'b_kvc', 'W_cproj', 'b_cproj', 'W_mlp1', 'b_mlp1', 'W_mlp2', 'b_mlp2')}
    del _L0_xcond_all

    def _L1_xcond_setup():
        import jax, jax.numpy as jnp
        import numpy as np
        D = 128
        H = 16
        DH = D // H
        DFF = 512
        B = 2
        L = 256
        EPS = 1e-05

        def layer_norm(x, g, b):
            mu = jnp.mean(x, axis=-1, keepdims=True)
            var = jnp.mean(jnp.square(x - mu), axis=-1, keepdims=True)
            return (x - mu) * jax.lax.rsqrt(var + EPS) * g + b

        def ada_ln(x, t_emb, ln_g, ln_b, aff_w, aff_b):
            normed = layer_norm(x, ln_g, ln_b)
            affine = t_emb @ aff_w + aff_b
            gamma, beta = jnp.split(affine, 2, axis=-1)
            return gamma[:, None, :] * normed + beta[:, None, :]

        def mha(q_in, k_in, v_in, qw, qb, kw, kb, vw, vb, ow, ob):
            Bq, Lq, _ = q_in.shape
            Lk = k_in.shape[1]
            Q = (q_in @ qw + qb).reshape(Bq, Lq, H, DH)
            K = (k_in @ kw + kb).reshape(Bq, Lk, H, DH)
            V = (v_in @ vw + vb).reshape(Bq, Lk, H, DH)
            scores = jnp.einsum('bqhd,bkhd->bhqk', Q, K) / np.sqrt(DH).astype(np.float32)
            attn = jax.nn.softmax(scores, axis=-1)
            out = jnp.einsum('bhqk,bkhd->bqhd', attn, V).reshape(Bq, Lq, D)
            return out @ ow + ob
        key = jax.random.key(seed)
        ks = jax.random.split(key, 32)
        s = lambda k, shape, scale=0.02: jax.random.normal(k, shape, dtype=jnp.float32) * scale
        inp = {'x': jax.random.normal(ks[0], (B, L, D), dtype=jnp.float32), 'u': jax.random.normal(ks[1], (B, L, D), dtype=jnp.float32), 't_emb': jax.random.normal(ks[2], (B, D), dtype=jnp.float32), 'ln1_g': jnp.ones((D,), jnp.float32), 'ln1_b': jnp.zeros((D,), jnp.float32), 'aff1_w': s(ks[3], (D, 2 * D)), 'aff1_b': jnp.zeros((2 * D,), jnp.float32), 'ln2_g': jnp.ones((D,), jnp.float32), 'ln2_b': jnp.zeros((D,), jnp.float32), 'aff2_w': s(ks[4], (D, 2 * D)), 'aff2_b': jnp.zeros((2 * D,), jnp.float32), 'sa_qw': s(ks[5], (D, D)), 'sa_qb': jnp.zeros((D,), jnp.float32), 'sa_kw': s(ks[6], (D, D)), 'sa_kb': jnp.zeros((D,), jnp.float32), 'sa_vw': s(ks[7], (D, D)), 'sa_vb': jnp.zeros((D,), jnp.float32), 'sa_ow': s(ks[8], (D, D)), 'sa_ob': jnp.zeros((D,), jnp.float32), 'ca_qw': s(ks[9], (D, D)), 'ca_qb': jnp.zeros((D,), jnp.float32), 'ca_kw': s(ks[10], (D, D)), 'ca_kb': jnp.zeros((D,), jnp.float32), 'ca_vw': s(ks[11], (D, D)), 'ca_vb': jnp.zeros((D,), jnp.float32), 'ca_ow': s(ks[12], (D, D)), 'ca_ob': jnp.zeros((D,), jnp.float32), 'ffn_w1': s(ks[13], (D, DFF)), 'ffn_b1': jnp.zeros((DFF,), jnp.float32), 'ffn_w2': s(ks[14], (DFF, D)), 'ffn_b2': jnp.zeros((D,), jnp.float32)}
        return inp
    _L1_xcond_all = _L1_xcond_setup()
    _L1_xcond_in = {k: v for k, v in _L1_xcond_all.items() if k in ('ln1_g', 'ln1_b', 'aff1_w', 'aff1_b', 'ln2_g', 'ln2_b', 'aff2_w', 'aff2_b', 'sa_qw', 'sa_qb', 'sa_kw', 'sa_kb', 'sa_vw', 'sa_vb', 'sa_ow', 'sa_ob', 'ca_qw', 'ca_qb', 'ca_kw', 'ca_kb', 'ca_vw', 'ca_vb', 'ca_ow', 'ca_ob', 'ffn_w1', 'ffn_b1', 'ffn_w2', 'ffn_b2')}
    del _L1_xcond_all

    def _L2_xcond_setup():
        import jax, jax.numpy as jnp
        import numpy as np
        H = 128
        RH = 2 * H
        E = 3
        B, T, P = (8, 256, 64)
        LN_EPS = 1e-05

        def _layer_norm(x, gamma, beta):
            mu = jnp.mean(x, axis=-1, keepdims=True)
            var = jnp.mean(jnp.square(x - mu), axis=-1, keepdims=True)
            return (x - mu) * jax.lax.rsqrt(var + LN_EPS) * gamma + beta
        key = jax.random.key(seed)
        ks = jax.random.split(key, 24)
        s = lambda fan_in: 1.0 / np.sqrt(fan_in)
        inp = {'mix_hidden_states': jax.random.normal(ks[0], (B, T, H), jnp.float32), 'global_anchor': jax.random.normal(ks[1], (B, H), jnp.float32), 'prototype_bank': jax.random.normal(ks[2], (B, P, H), jnp.float32), 'ln_gamma': jnp.ones((H,), jnp.float32), 'ln_beta': jnp.zeros((H,), jnp.float32), 'Wq': jax.random.normal(ks[3], (H, H), jnp.float32) * s(H), 'Wk': jax.random.normal(ks[4], (H, H), jnp.float32) * s(H), 'Wv': jax.random.normal(ks[5], (H, H), jnp.float32) * s(H), 'router_W': jax.random.normal(ks[6], (3 * H, E), jnp.float32) * s(3 * H), 'router_b': jnp.zeros((E,), jnp.float32), 'e_w1': jax.random.normal(ks[7], (E, 3 * H, RH), jnp.float32) * s(3 * H), 'e_b1': jnp.zeros((E, RH), jnp.float32), 'e_w2': jax.random.normal(ks[8], (E, RH, H), jnp.float32) * s(RH), 'e_b2': jnp.zeros((E, H), jnp.float32), 'gate_w1': jax.random.normal(ks[9], (3 * H, H), jnp.float32) * s(3 * H), 'gate_b1': jnp.zeros((H,), jnp.float32), 'gate_w2': jax.random.normal(ks[10], (H, H), jnp.float32) * s(H), 'gate_b2': jnp.zeros((H,), jnp.float32), 'out_w': jax.random.normal(ks[11], (H, H), jnp.float32) * s(H), 'out_b': jnp.zeros((H,), jnp.float32)}
        return inp
    _L2_xcond_all = _L2_xcond_setup()
    _L2_xcond_in = {k: v for k, v in _L2_xcond_all.items() if k in ('ln_gamma', 'ln_beta', 'Wq', 'Wk', 'Wv', 'router_W', 'router_b', 'e_w1', 'e_b1', 'e_w2', 'e_b2', 'gate_w1', 'gate_b1', 'gate_w2', 'gate_b2', 'out_w', 'out_b')}
    del _L2_xcond_all

    def _L3_xcond_setup():
        import jax, jax.numpy as jnp
        import numpy as np
        D = 128
        H = 16
        HD = D // H
        MLP = 4 * D
        EPS = 1e-06
        SCALE = HD ** (-0.5)

        def _p(key, shape, s=0.02):
            return jax.random.normal(key, shape, dtype=jnp.float32) * s

        def _ln(x):
            mu = jnp.mean(x, axis=-1, keepdims=True)
            var = jnp.var(x, axis=-1, keepdims=True)
            return (x - mu) * jax.lax.rsqrt(var + EPS)

        def _heads(t):
            B, L, _ = t.shape
            return t.reshape(B, L, H, HD).transpose(0, 2, 1, 3)

        def _attend(q, k, v):
            attn = jnp.einsum('bhnd,bhsd->bhns', q, k) * SCALE
            attn = jax.nn.softmax(attn, axis=-1)
            o = jnp.einsum('bhns,bhsd->bhnd', attn, v)
            B, _, N, _ = q.shape
            return o.transpose(0, 2, 1, 3).reshape(B, N, D)
        key = jax.random.key(seed)
        ks = jax.random.split(key, 24)
        B, N, S = (4, 128, 77)
        return {'x': jax.random.normal(ks[0], (B, N, D), dtype=jnp.float32), 't_emb': jax.random.normal(ks[1], (B, D), dtype=jnp.float32), 'context': jax.random.normal(ks[2], (B, S, D), dtype=jnp.float32), 'adaln_w': _p(ks[3], (D, 6 * D)), 'adaln_b': _p(ks[4], (6 * D,)), 'qkv_w': _p(ks[5], (D, 3 * D)), 'qkv_b': _p(ks[6], (3 * D,)), 'sa_proj_w': _p(ks[7], (D, D)), 'sa_proj_b': _p(ks[8], (D,)), 'q_w': _p(ks[9], (D, D)), 'q_b': _p(ks[10], (D,)), 'kv_w': _p(ks[11], (D, 2 * D)), 'kv_b': _p(ks[12], (2 * D,)), 'ca_proj_w': _p(ks[13], (D, D)), 'ca_proj_b': _p(ks[14], (D,)), 'fc1_w': _p(ks[15], (D, MLP)), 'fc1_b': _p(ks[16], (MLP,)), 'fc2_w': _p(ks[17], (MLP, D)), 'fc2_b': _p(ks[18], (D,))}
    _L3_xcond_all = _L3_xcond_setup()
    _L3_xcond_in = {k: v for k, v in _L3_xcond_all.items() if k in ('adaln_w', 'adaln_b', 'qkv_w', 'qkv_b', 'sa_proj_w', 'sa_proj_b', 'q_w', 'q_b', 'kv_w', 'kv_b', 'ca_proj_w', 'ca_proj_b', 'fc1_w', 'fc1_b', 'fc2_w', 'fc2_b')}
    del _L3_xcond_all
    return {'x': x, 'cond_1024': cond_1024, 'ctx_1024': ctx_1024, 'L0_xcond_W_mod': _L0_xcond_in['W_mod'], 'L0_xcond_b_mod': _L0_xcond_in['b_mod'], 'L0_xcond_W_qkv': _L0_xcond_in['W_qkv'], 'L0_xcond_b_qkv': _L0_xcond_in['b_qkv'], 'L0_xcond_W_proj': _L0_xcond_in['W_proj'], 'L0_xcond_b_proj': _L0_xcond_in['b_proj'], 'L0_xcond_W_qc': _L0_xcond_in['W_qc'], 'L0_xcond_b_qc': _L0_xcond_in['b_qc'], 'L0_xcond_W_kvc': _L0_xcond_in['W_kvc'], 'L0_xcond_b_kvc': _L0_xcond_in['b_kvc'], 'L0_xcond_W_cproj': _L0_xcond_in['W_cproj'], 'L0_xcond_b_cproj': _L0_xcond_in['b_cproj'], 'L0_xcond_W_mlp1': _L0_xcond_in['W_mlp1'], 'L0_xcond_b_mlp1': _L0_xcond_in['b_mlp1'], 'L0_xcond_W_mlp2': _L0_xcond_in['W_mlp2'], 'L0_xcond_b_mlp2': _L0_xcond_in['b_mlp2'], 'L1_xcond_ln1_g': _L1_xcond_in['ln1_g'], 'L1_xcond_ln1_b': _L1_xcond_in['ln1_b'], 'L1_xcond_aff1_w': _L1_xcond_in['aff1_w'], 'L1_xcond_aff1_b': _L1_xcond_in['aff1_b'], 'L1_xcond_ln2_g': _L1_xcond_in['ln2_g'], 'L1_xcond_ln2_b': _L1_xcond_in['ln2_b'], 'L1_xcond_aff2_w': _L1_xcond_in['aff2_w'], 'L1_xcond_aff2_b': _L1_xcond_in['aff2_b'], 'L1_xcond_sa_qw': _L1_xcond_in['sa_qw'], 'L1_xcond_sa_qb': _L1_xcond_in['sa_qb'], 'L1_xcond_sa_kw': _L1_xcond_in['sa_kw'], 'L1_xcond_sa_kb': _L1_xcond_in['sa_kb'], 'L1_xcond_sa_vw': _L1_xcond_in['sa_vw'], 'L1_xcond_sa_vb': _L1_xcond_in['sa_vb'], 'L1_xcond_sa_ow': _L1_xcond_in['sa_ow'], 'L1_xcond_sa_ob': _L1_xcond_in['sa_ob'], 'L1_xcond_ca_qw': _L1_xcond_in['ca_qw'], 'L1_xcond_ca_qb': _L1_xcond_in['ca_qb'], 'L1_xcond_ca_kw': _L1_xcond_in['ca_kw'], 'L1_xcond_ca_kb': _L1_xcond_in['ca_kb'], 'L1_xcond_ca_vw': _L1_xcond_in['ca_vw'], 'L1_xcond_ca_vb': _L1_xcond_in['ca_vb'], 'L1_xcond_ca_ow': _L1_xcond_in['ca_ow'], 'L1_xcond_ca_ob': _L1_xcond_in['ca_ob'], 'L1_xcond_ffn_w1': _L1_xcond_in['ffn_w1'], 'L1_xcond_ffn_b1': _L1_xcond_in['ffn_b1'], 'L1_xcond_ffn_w2': _L1_xcond_in['ffn_w2'], 'L1_xcond_ffn_b2': _L1_xcond_in['ffn_b2'], 'L2_xcond_ln_gamma': _L2_xcond_in['ln_gamma'], 'L2_xcond_ln_beta': _L2_xcond_in['ln_beta'], 'L2_xcond_Wq': _L2_xcond_in['Wq'], 'L2_xcond_Wk': _L2_xcond_in['Wk'], 'L2_xcond_Wv': _L2_xcond_in['Wv'], 'L2_xcond_router_W': _L2_xcond_in['router_W'], 'L2_xcond_router_b': _L2_xcond_in['router_b'], 'L2_xcond_e_w1': _L2_xcond_in['e_w1'], 'L2_xcond_e_b1': _L2_xcond_in['e_b1'], 'L2_xcond_e_w2': _L2_xcond_in['e_w2'], 'L2_xcond_e_b2': _L2_xcond_in['e_b2'], 'L2_xcond_gate_w1': _L2_xcond_in['gate_w1'], 'L2_xcond_gate_b1': _L2_xcond_in['gate_b1'], 'L2_xcond_gate_w2': _L2_xcond_in['gate_w2'], 'L2_xcond_gate_b2': _L2_xcond_in['gate_b2'], 'L2_xcond_out_w': _L2_xcond_in['out_w'], 'L2_xcond_out_b': _L2_xcond_in['out_b'], 'L3_xcond_adaln_w': _L3_xcond_in['adaln_w'], 'L3_xcond_adaln_b': _L3_xcond_in['adaln_b'], 'L3_xcond_qkv_w': _L3_xcond_in['qkv_w'], 'L3_xcond_qkv_b': _L3_xcond_in['qkv_b'], 'L3_xcond_sa_proj_w': _L3_xcond_in['sa_proj_w'], 'L3_xcond_sa_proj_b': _L3_xcond_in['sa_proj_b'], 'L3_xcond_q_w': _L3_xcond_in['q_w'], 'L3_xcond_q_b': _L3_xcond_in['q_b'], 'L3_xcond_kv_w': _L3_xcond_in['kv_w'], 'L3_xcond_kv_b': _L3_xcond_in['kv_b'], 'L3_xcond_ca_proj_w': _L3_xcond_in['ca_proj_w'], 'L3_xcond_ca_proj_b': _L3_xcond_in['ca_proj_b'], 'L3_xcond_fc1_w': _L3_xcond_in['fc1_w'], 'L3_xcond_fc1_b': _L3_xcond_in['fc1_b'], 'L3_xcond_fc2_w': _L3_xcond_in['fc2_w'], 'L3_xcond_fc2_b': _L3_xcond_in['fc2_b']}

def reference(x, cond_1024, ctx_1024, L0_xcond_W_mod, L0_xcond_b_mod, L0_xcond_W_qkv, L0_xcond_b_qkv, L0_xcond_W_proj, L0_xcond_b_proj, L0_xcond_W_qc, L0_xcond_b_qc, L0_xcond_W_kvc, L0_xcond_b_kvc, L0_xcond_W_cproj, L0_xcond_b_cproj, L0_xcond_W_mlp1, L0_xcond_b_mlp1, L0_xcond_W_mlp2, L0_xcond_b_mlp2, L1_xcond_ln1_g, L1_xcond_ln1_b, L1_xcond_aff1_w, L1_xcond_aff1_b, L1_xcond_ln2_g, L1_xcond_ln2_b, L1_xcond_aff2_w, L1_xcond_aff2_b, L1_xcond_sa_qw, L1_xcond_sa_qb, L1_xcond_sa_kw, L1_xcond_sa_kb, L1_xcond_sa_vw, L1_xcond_sa_vb, L1_xcond_sa_ow, L1_xcond_sa_ob, L1_xcond_ca_qw, L1_xcond_ca_qb, L1_xcond_ca_kw, L1_xcond_ca_kb, L1_xcond_ca_vw, L1_xcond_ca_vb, L1_xcond_ca_ow, L1_xcond_ca_ob, L1_xcond_ffn_w1, L1_xcond_ffn_b1, L1_xcond_ffn_w2, L1_xcond_ffn_b2, L2_xcond_ln_gamma, L2_xcond_ln_beta, L2_xcond_Wq, L2_xcond_Wk, L2_xcond_Wv, L2_xcond_router_W, L2_xcond_router_b, L2_xcond_e_w1, L2_xcond_e_b1, L2_xcond_e_w2, L2_xcond_e_b2, L2_xcond_gate_w1, L2_xcond_gate_b1, L2_xcond_gate_w2, L2_xcond_gate_b2, L2_xcond_out_w, L2_xcond_out_b, L3_xcond_adaln_w, L3_xcond_adaln_b, L3_xcond_qkv_w, L3_xcond_qkv_b, L3_xcond_sa_proj_w, L3_xcond_sa_proj_b, L3_xcond_q_w, L3_xcond_q_b, L3_xcond_kv_w, L3_xcond_kv_b, L3_xcond_ca_proj_w, L3_xcond_ca_proj_b, L3_xcond_fc1_w, L3_xcond_fc1_b, L3_xcond_fc2_w, L3_xcond_fc2_b):
    import jax
    import jax.numpy as jnp

    def _L0_xcond_ref(x, c, context, W_mod, b_mod, W_qkv, b_qkv, W_proj, b_proj, W_qc, b_qc, W_kvc, b_kvc, W_cproj, b_cproj, W_mlp1, b_mlp1, W_mlp2, b_mlp2):
        import jax, jax.numpy as jnp
        import numpy as np
        LN_EPS = 1e-06

        def _ln(x):
            mu = jnp.mean(x, axis=-1, keepdims=True)
            var = jnp.var(x, axis=-1, keepdims=True)
            return (x - mu) * jax.lax.rsqrt(var + LN_EPS)
        B, N, H = x.shape
        NH = 16
        hd = H // NH
        scale = hd ** (-0.5)
        c_proj = jax.nn.silu(c) @ W_mod + b_mod
        shift_a, scale_a, gate_a, shift_m, scale_m, gate_m = jnp.split(c_proj, 6, axis=-1)

        def modulate(t, shift, sc):
            return t * (1 + sc[:, None]) + shift[:, None]
        x_norm = modulate(_ln(x), shift_a, scale_a)
        qkv = x_norm @ W_qkv + b_qkv
        q, k, v = jnp.split(qkv, 3, axis=-1)
        q = q.reshape(B, N, NH, hd).transpose(0, 2, 1, 3)
        k = k.reshape(B, N, NH, hd).transpose(0, 2, 1, 3)
        v = v.reshape(B, N, NH, hd).transpose(0, 2, 1, 3)
        attn_w = jax.nn.softmax(jnp.einsum('bhqd,bhkd->bhqk', q, k) * scale, axis=-1)
        attn_out = jnp.einsum('bhqk,bhkd->bhqd', attn_w, v)
        attn_out = attn_out.transpose(0, 2, 1, 3).reshape(B, N, H)
        attn_out = attn_out @ W_proj + b_proj
        x = x + gate_a[:, None] * attn_out
        S = context.shape[1]
        q_c = _ln(x) @ W_qc + b_qc
        kv_c = _ln(context) @ W_kvc + b_kvc
        k_c, v_c = jnp.split(kv_c, 2, axis=-1)
        q_c = q_c.reshape(B, N, NH, hd).transpose(0, 2, 1, 3)
        k_c = k_c.reshape(B, S, NH, hd).transpose(0, 2, 1, 3)
        v_c = v_c.reshape(B, S, NH, hd).transpose(0, 2, 1, 3)
        c_attn_w = jax.nn.softmax(jnp.einsum('bhqd,bhsd->bhqs', q_c, k_c) * scale, axis=-1)
        c_attn_out = jnp.einsum('bhqs,bhsd->bhqd', c_attn_w, v_c)
        c_attn_out = c_attn_out.transpose(0, 2, 1, 3).reshape(B, N, H)
        c_attn_out = c_attn_out @ W_cproj + b_cproj
        x = x + c_attn_out
        x_norm2 = modulate(_ln(x), shift_m, scale_m)
        h = jax.nn.gelu(x_norm2 @ W_mlp1 + b_mlp1)
        h = h @ W_mlp2 + b_mlp2
        x = x + gate_m[:, None] * h
        return x

    def _L1_xcond_ref(x, u, t_emb, ln1_g, ln1_b, aff1_w, aff1_b, ln2_g, ln2_b, aff2_w, aff2_b, sa_qw, sa_qb, sa_kw, sa_kb, sa_vw, sa_vb, sa_ow, sa_ob, ca_qw, ca_qb, ca_kw, ca_kb, ca_vw, ca_vb, ca_ow, ca_ob, ffn_w1, ffn_b1, ffn_w2, ffn_b2):
        import jax, jax.numpy as jnp
        import numpy as np
        D = 128
        H = 16
        DH = D // H
        DFF = 512
        B = 2
        L = 256
        EPS = 1e-05

        def layer_norm(x, g, b):
            mu = jnp.mean(x, axis=-1, keepdims=True)
            var = jnp.mean(jnp.square(x - mu), axis=-1, keepdims=True)
            return (x - mu) * jax.lax.rsqrt(var + EPS) * g + b

        def ada_ln(x, t_emb, ln_g, ln_b, aff_w, aff_b):
            normed = layer_norm(x, ln_g, ln_b)
            affine = t_emb @ aff_w + aff_b
            gamma, beta = jnp.split(affine, 2, axis=-1)
            return gamma[:, None, :] * normed + beta[:, None, :]

        def mha(q_in, k_in, v_in, qw, qb, kw, kb, vw, vb, ow, ob):
            Bq, Lq, _ = q_in.shape
            Lk = k_in.shape[1]
            Q = (q_in @ qw + qb).reshape(Bq, Lq, H, DH)
            K = (k_in @ kw + kb).reshape(Bq, Lk, H, DH)
            V = (v_in @ vw + vb).reshape(Bq, Lk, H, DH)
            scores = jnp.einsum('bqhd,bkhd->bhqk', Q, K) / np.sqrt(DH).astype(np.float32)
            attn = jax.nn.softmax(scores, axis=-1)
            out = jnp.einsum('bhqk,bkhd->bqhd', attn, V).reshape(Bq, Lq, D)
            return out @ ow + ob
        xn = ada_ln(x, t_emb, ln1_g, ln1_b, aff1_w, aff1_b)
        x = x + mha(xn, xn, xn, sa_qw, sa_qb, sa_kw, sa_kb, sa_vw, sa_vb, sa_ow, sa_ob)
        x = x + mha(x, u, u, ca_qw, ca_qb, ca_kw, ca_kb, ca_vw, ca_vb, ca_ow, ca_ob)
        xn = ada_ln(x, t_emb, ln2_g, ln2_b, aff2_w, aff2_b)
        h = jax.nn.gelu(xn @ ffn_w1 + ffn_b1, approximate=False)
        x = x + (h @ ffn_w2 + ffn_b2)
        return x

    def _L2_xcond_ref(mix_hidden_states, global_anchor, prototype_bank, ln_gamma, ln_beta, Wq, Wk, Wv, router_W, router_b, e_w1, e_b1, e_w2, e_b2, gate_w1, gate_b1, gate_w2, gate_b2, out_w, out_b):
        import jax, jax.numpy as jnp
        import numpy as np
        H = 128
        RH = 2 * H
        E = 3
        B, T, P = (8, 256, 64)
        LN_EPS = 1e-05

        def _layer_norm(x, gamma, beta):
            mu = jnp.mean(x, axis=-1, keepdims=True)
            var = jnp.mean(jnp.square(x - mu), axis=-1, keepdims=True)
            return (x - mu) * jax.lax.rsqrt(var + LN_EPS) * gamma + beta
        x = mix_hidden_states
        nx = _layer_norm(x, ln_gamma, ln_beta)
        q = nx @ Wq
        k = prototype_bank @ Wk
        v = prototype_bank @ Wv
        scores = jnp.einsum('bth,bph->btp', q, k) * H ** (-0.5)
        weights = jax.nn.softmax(scores, axis=-1)
        evidence = jnp.einsum('btp,bph->bth', weights, v)
        anchor = jnp.broadcast_to(global_anchor[:, None, :], nx.shape)
        combined = jnp.concatenate([nx, evidence, anchor], axis=-1)
        router_logits = combined @ router_W + router_b
        router_probs = jax.nn.softmax(router_logits, axis=-1)
        h = jax.nn.silu(jnp.einsum('btc,ecr->bter', combined, e_w1) + e_b1)
        expert_out = jnp.einsum('bter,erh->bteh', h, e_w2) + e_b2
        routed = jnp.sum(expert_out * router_probs[..., None], axis=-2)
        g = jax.nn.sigmoid(jax.nn.silu(combined @ gate_w1 + gate_b1) @ gate_w2 + gate_b2)
        refined_delta = g * (routed @ out_w + out_b)
        return x + refined_delta

    def _L3_xcond_ref(x, t_emb, context, adaln_w, adaln_b, qkv_w, qkv_b, sa_proj_w, sa_proj_b, q_w, q_b, kv_w, kv_b, ca_proj_w, ca_proj_b, fc1_w, fc1_b, fc2_w, fc2_b):
        import jax, jax.numpy as jnp
        import numpy as np
        D = 128
        H = 16
        HD = D // H
        MLP = 4 * D
        EPS = 1e-06
        SCALE = HD ** (-0.5)

        def _p(key, shape, s=0.02):
            return jax.random.normal(key, shape, dtype=jnp.float32) * s

        def _ln(x):
            mu = jnp.mean(x, axis=-1, keepdims=True)
            var = jnp.var(x, axis=-1, keepdims=True)
            return (x - mu) * jax.lax.rsqrt(var + EPS)

        def _heads(t):
            B, L, _ = t.shape
            return t.reshape(B, L, H, HD).transpose(0, 2, 1, 3)

        def _attend(q, k, v):
            attn = jnp.einsum('bhnd,bhsd->bhns', q, k) * SCALE
            attn = jax.nn.softmax(attn, axis=-1)
            o = jnp.einsum('bhns,bhsd->bhnd', attn, v)
            B, _, N, _ = q.shape
            return o.transpose(0, 2, 1, 3).reshape(B, N, D)
        B, N, _ = x.shape
        S = context.shape[1]
        mod = jax.nn.silu(t_emb) @ adaln_w + adaln_b
        sh_sa, sc_sa, g_sa, sh_ff, sc_ff, g_ff = jnp.split(mod[:, None, :], 6, axis=-1)
        xm = _ln(x) * (1.0 + sc_sa) + sh_sa
        qkv = (xm @ qkv_w + qkv_b).reshape(B, N, 3, H, HD)
        q = qkv[:, :, 0].transpose(0, 2, 1, 3)
        k = qkv[:, :, 1].transpose(0, 2, 1, 3)
        v = qkv[:, :, 2].transpose(0, 2, 1, 3)
        x_sa = _attend(q, k, v) @ sa_proj_w + sa_proj_b
        x = x + g_sa * x_sa
        xn = _ln(x)
        q = _heads(xn @ q_w + q_b)
        kv = (context @ kv_w + kv_b).reshape(B, S, 2, H, HD)
        k = kv[:, :, 0].transpose(0, 2, 1, 3)
        v = kv[:, :, 1].transpose(0, 2, 1, 3)
        x_ca = _attend(q, k, v) @ ca_proj_w + ca_proj_b
        x = x + x_ca
        xm = _ln(x) * (1.0 + sc_ff) + sh_ff
        h = jax.nn.gelu(xm @ fc1_w + fc1_b, approximate=True)
        x_ff = h @ fc2_w + fc2_b
        x = x + g_ff * x_ff
        return x
    x = _L0_xcond_ref(x, cond_1024, ctx_1024, L0_xcond_W_mod, L0_xcond_b_mod, L0_xcond_W_qkv, L0_xcond_b_qkv, L0_xcond_W_proj, L0_xcond_b_proj, L0_xcond_W_qc, L0_xcond_b_qc, L0_xcond_W_kvc, L0_xcond_b_kvc, L0_xcond_W_cproj, L0_xcond_b_cproj, L0_xcond_W_mlp1, L0_xcond_b_mlp1, L0_xcond_W_mlp2, L0_xcond_b_mlp2)
    x = _L1_xcond_ref(x, ctx_1024, cond_1024, L1_xcond_ln1_g, L1_xcond_ln1_b, L1_xcond_aff1_w, L1_xcond_aff1_b, L1_xcond_ln2_g, L1_xcond_ln2_b, L1_xcond_aff2_w, L1_xcond_aff2_b, L1_xcond_sa_qw, L1_xcond_sa_qb, L1_xcond_sa_kw, L1_xcond_sa_kb, L1_xcond_sa_vw, L1_xcond_sa_vb, L1_xcond_sa_ow, L1_xcond_sa_ob, L1_xcond_ca_qw, L1_xcond_ca_qb, L1_xcond_ca_kw, L1_xcond_ca_kb, L1_xcond_ca_vw, L1_xcond_ca_vb, L1_xcond_ca_ow, L1_xcond_ca_ob, L1_xcond_ffn_w1, L1_xcond_ffn_b1, L1_xcond_ffn_w2, L1_xcond_ffn_b2)
    x = _L2_xcond_ref(x, cond_1024, ctx_1024, L2_xcond_ln_gamma, L2_xcond_ln_beta, L2_xcond_Wq, L2_xcond_Wk, L2_xcond_Wv, L2_xcond_router_W, L2_xcond_router_b, L2_xcond_e_w1, L2_xcond_e_b1, L2_xcond_e_w2, L2_xcond_e_b2, L2_xcond_gate_w1, L2_xcond_gate_b1, L2_xcond_gate_w2, L2_xcond_gate_b2, L2_xcond_out_w, L2_xcond_out_b)
    x = _L3_xcond_ref(x, cond_1024, ctx_1024, L3_xcond_adaln_w, L3_xcond_adaln_b, L3_xcond_qkv_w, L3_xcond_qkv_b, L3_xcond_sa_proj_w, L3_xcond_sa_proj_b, L3_xcond_q_w, L3_xcond_q_b, L3_xcond_kv_w, L3_xcond_kv_b, L3_xcond_ca_proj_w, L3_xcond_ca_proj_b, L3_xcond_fc1_w, L3_xcond_fc1_b, L3_xcond_fc2_w, L3_xcond_fc2_b)
    return x

_drawn_inputs = setup_inputs


def setup_inputs(seed=0):
    import zlib

    import numpy as np

    out = dict(_drawn_inputs(seed))
    spreads = {'L0_xcond_b_mod': (0.0, 0.1),
     'L0_xcond_b_qkv': (0.0, 0.1),
     'L0_xcond_b_proj': (0.0, 0.1),
     'L0_xcond_b_qc': (0.0, 0.544),
     'L0_xcond_b_kvc': (0.0, 0.1),
     'L0_xcond_b_cproj': (0.0, 0.1),
     'L0_xcond_b_mlp1': (0.0, 0.1),
     'L0_xcond_b_mlp2': (0.0, 0.1),
     'L1_xcond_ln1_g': (1.0, 0.6),
     'L1_xcond_ln1_b': (0.0, 0.8),
     'L1_xcond_aff1_b': (0.0, 0.8),
     'L1_xcond_ln2_g': (1.0, 0.6),
     'L1_xcond_ln2_b': (0.0, 0.8),
     'L1_xcond_aff2_b': (0.0, 0.8),
     'L1_xcond_sa_qb': (0.0, 0.8),
     'L1_xcond_sa_kb': (0.0, 2.0),
     'L1_xcond_sa_vb': (0.0, 0.525),
     'L1_xcond_sa_ob': (0.0, 0.1),
     'L1_xcond_ca_qb': (0.0, 2.0),
     'L1_xcond_ca_kb': (0.0, 2.0),
     'L1_xcond_ca_vb': (0.0, 0.513),
     'L1_xcond_ca_ob': (0.0, 0.1),
     'L1_xcond_ffn_b1': (0.0, 0.461),
     'L1_xcond_ffn_b2': (0.0, 0.1),
     'L2_xcond_ln_gamma': (1.0, 0.6),
     'L2_xcond_ln_beta': (0.0, 0.8),
     'L2_xcond_router_b': (0.0, 0.8),
     'L2_xcond_e_b1': (0.0, 0.506),
     'L2_xcond_e_b2': (0.0, 0.304),
     'L2_xcond_gate_b1': (0.0, 2.0),
     'L2_xcond_gate_b2': (0.0, 0.8),
     'L2_xcond_out_b': (0.0, 0.442)}
    factors = {'L1_xcond_aff1_w': 5.856,
     'L1_xcond_aff2_w': 4.386,
     'L1_xcond_sa_qw': 8.0,
     'L1_xcond_sa_kw': 8.0,
     'L1_xcond_sa_vw': 5.343,
     'L1_xcond_sa_ow': 2.937,
     'L1_xcond_ca_qw': 8.0,
     'L1_xcond_ca_kw': 8.0,
     'L1_xcond_ca_vw': 2.983,
     'L1_xcond_ffn_w1': 4.024,
     'L3_xcond_adaln_w': 8.0,
     'L3_xcond_adaln_b': 8.0,
     'L3_xcond_qkv_w': 8.0,
     'L3_xcond_qkv_b': 8.0,
     'L3_xcond_sa_proj_w': 8.0,
     'L3_xcond_sa_proj_b': 8.0,
     'L3_xcond_q_w': 28.702,
     'L3_xcond_q_b': 200.0,
     'L3_xcond_kv_w': 2.967,
     'L3_xcond_kv_b': 37.07,
     'L3_xcond_ca_proj_w': 2.972,
     'L3_xcond_ca_proj_b': 23.484,
     'L3_xcond_fc1_w': 8.0,
     'L3_xcond_fc1_b': 8.0,
     'L3_xcond_fc2_w': 8.0,
     'L3_xcond_fc2_b': 31.487}
    for name, (base, spread) in spreads.items():
        noise = np.random.default_rng([zlib.crc32(name.encode()), seed]).standard_normal(out[name].shape)
        drawn = base * np.exp(spread * noise) if base else spread * noise
        out[name] = jnp.asarray(drawn.astype(out[name].dtype))
    for name, factor in factors.items():
        out[name] = (out[name] * factor).astype(out[name].dtype)
    return out
```

```python
import concourse.bass as bass
from concourse import mybir
from contextlib import ExitStack

F32 = mybir.dt.float32
BF16 = mybir.dt.bfloat16
ACT = mybir.ActivationFunctionType
ALU = mybir.AluOpType
AX = mybir.AxisListType

P = 128
B = 32
N = 100
S = 1444
T = B * N
HEADS = 16
HD = P // HEADS
CH = 4 * N
NCH = T // CH
BANK = 512
KTS = [min(128, S - k) for k in range(0, S, 128)]
PAIRS = HEADS // 2
Q_PARTS = (0, 0, 1, 1, 0, 2)
K_PARTS = (0, 1, 0, 1, 2, 0)
SLOTS = len(Q_PARTS)
SROWS = 16 * SLOTS
MROWS = 6
ROWS = SROWS + MROWS
VW = HD + 1
SCALE = float(HD) ** -0.5
UNROLL = 4
LAG = 3


class Ctx:
    pass


def wait(eng, sem, value):
    if isinstance(value, int) and value <= 0:
        return
    eng.wait_ge(sem, value)


class Batch:

    def __init__(self, i, off, lag):
        self.i, self.off, self.lag = i, off, lag
        self.b, self.s, self.r = i * lag + off, off % lag, i + off // lag

    def prev(self):
        return Batch(self.i, self.off - 1, self.lag)


def tok(buf, c, n=CH):
    return buf[:, bass.ds(c * n, n)]


def bank(g, c):
    return g.ps[:, bass.ds(c * BANK, CH)]



def chunks(eng):
    with eng.Fori(0, NCH // UNROLL) as i:
        for u in range(UNROLL):
            yield i * UNROLL + u


def batches_of(c):
    return [c * (CH // N) + j for j in range(CH // N)]


def pe_linear(g, pe, weights, sources, ready, per, free, full):
    for c in chunks(pe):
        if ready is not None:
            pe.wait_ge(ready, per * (c + 1))
        if free is not None:
            pe.wait_ge(free, c + 1)
        for k, (w, src) in enumerate(zip(weights, sources)):
            ins = g.nc.tensor.matmul(bank(g, c), w, src(c), start=(k == 0), stop=(k == len(weights) - 1))
        ins.then_inc(full, 1)


def dve_center(g, dve, src, xc, mean_full, centered):
    for c in chunks(dve):
        dve.wait_ge(mean_full, c + 1)
        g.nc.vector.tensor_tensor(tok(xc, c), tok(src, c), bank(g, c), ALU.subtract).then_inc(centered, 1)


def act_square(g, act, xc, sq, centered, squared):
    for c in chunks(act):
        act.wait_ge(centered, c + 1)
        g.nc.scalar.activation(tok(sq, c), tok(xc, c), ACT.Square).then_inc(squared, 1)


def dve_variance(g, dve, sq, eps, var_full, var_read):
    for c in chunks(dve):
        dve.wait_ge(var_full, c + 1)
        g.nc.vector.tensor_scalar(tok(sq, c), bank(g, c), eps, None, ALU.add).then_inc(var_read, 1)


def act_std(g, act, sq, var_read, std_ready):
    for c in chunks(act):
        act.wait_ge(var_read, c + 1)
        g.nc.scalar.activation(tok(sq, c), tok(sq, c), ACT.Sqrt).then_inc(std_ready, 1)


def dve_rstd(g, dve, sq, std_ready, rstd_ready):
    for c in chunks(dve):
        dve.wait_ge(std_ready, c + 1)
        g.nc.vector.reciprocal(tok(sq, c), tok(sq, c)).then_inc(rstd_ready, 1)


def pool_normalize(g, pool, xc, sq, rstd_ready, normed):
    for c in chunks(pool):
        pool.wait_ge(rstd_ready, c + 1)
        g.nc.gpsimd.tensor_tensor(tok(xc, c), tok(xc, c), tok(sq, c), ALU.mult).then_inc(normed, 1)


def dve_modulate(g, dve, xn, mul, add, normed, modulated):
    for c in chunks(dve):
        dve.wait_ge(normed, c + 1)
        for b in batches_of(c):
            g.nc.vector.tensor_scalar(tok(xn, b, N), tok(xn, b, N), mul[:, bass.ds(b, 1)], add[:, bass.ds(b, 1)],
                                      ALU.mult, ALU.add).then_inc(modulated, 1)


def act_split(g, act, f, parts, f_ready, high, rest, middle):
    for c in chunks(act):
        act.wait_ge(f_ready, c + 1)
        g.nc.scalar.activation(parts[:, 0, bass.ds(c * CH, CH)], tok(f, c), ACT.Copy).then_inc(high, 1)
    for c in chunks(act):
        act.wait_ge(rest, c + 1)
        g.nc.scalar.activation(parts[:, 1, bass.ds(c * CH, CH)], tok(f, c), ACT.Copy).then_inc(middle, 1)


def pool_split(g, pool, f, parts, high, rest, middle, low):
    for c in chunks(pool):
        pool.wait_ge(high, c + 1)
        g.nc.gpsimd.tensor_tensor(tok(f, c), tok(f, c), parts[:, 0, bass.ds(c * CH, CH)],
                                  ALU.subtract).then_inc(rest, 1)
    for c in chunks(pool):
        pool.wait_ge(middle, c + 1)
        g.nc.gpsimd.tensor_tensor(parts[:, 2, bass.ds(c * CH, CH)], tok(f, c),
                                  parts[:, 1, bass.ds(c * CH, CH)], ALU.subtract).then_inc(low, 1)


def sp_parts_out(g, sp, parts, dram, low, stored):
    for c in chunks(sp):
        sp.wait_ge(low, c + 1)
        sp.dma_start(dram[:, :, bass.ds(c * CH, CH)], parts[:, :, bass.ds(c * CH, CH)]).then_inc(stored, 16)
    sp.wait_ge(stored, 16 * NCH)


def row(v):
    return v.rearrange("(k p) -> p k", p=P)


class Sems:

    def __init__(self, g, stack):
        self.g, self.made = g, []
        stack.callback(self.close)

    def __call__(self, name):
        g = self.g
        g.serial += 1
        self.made.append(g.nc.alloc_semaphore(f"{name}_{g.serial}"))
        return self.made[-1]

    def close(self):
        self.g.nc.clear_and_free_semaphores(self.made)
        self.g.nc.all_engine_barrier()



def setup_phase(g, x, cond):
    nc = g.nc
    with ExitStack() as st:
        sem = Sems(g, st)
        xin = st.enter_context(nc.sbuf_tensor("xin", [N, B, P], F32))
        cin = st.enter_context(nc.sbuf_tensor("cin", [B, P], F32))
        loaded, cleared, diag, consts = sem("x_loaded"), sem("cleared"), sem("diagonal"), sem("constants")
        turned, copied, cturned, ctanh, ccopied = sem("x_turned"), sem("x_copied"), sem("cond_turned"), sem("cond_tanh"), sem("cond_copied")
        PER = 4
        with nc.Block() as block:
            @block.sync
            def _(sp):
                sp.dma_start(xin[:, :, :], x.rearrange("b n p -> n b p")).then_inc(loaded, 16)
                sp.dma_start(cin[:, :], cond).then_inc(loaded, 16)

            @block.gpsimd
            def _(pool):
                nc.gpsimd.memset(g.ident[:, :], 0.0).then_inc(cleared, 1)
                pool.wait_ge(cleared, 1)
                nc.gpsimd.affine_select(out=g.ident[:, :], in_=g.ident[:, :], compare_op=ALU.not_equal, fill=1.0,
                                        base=0, pattern=[[-1, P]], channel_multiplier=1).then_inc(diag, 1)
                nc.gpsimd.memset(g.meaner[:, :], 1.0 / P).then_inc(consts, 1)
                nc.gpsimd.memset(g.zero[:, :], 0.0).then_inc(consts, 1)
                nc.gpsimd.memset(g.eps6[:, :], 1e-6).then_inc(consts, 1)

            @block.tensor
            def _(pe):
                pe.wait_ge(diag, 1)
                pe.wait_ge(loaded, 32)
                nc.tensor.transpose(g.ps[:, 7 * BANK:7 * BANK + B], cin[:, :], g.ident[0:B, 0:B]).then_inc(cturned, 1)
                pe.wait_ge(ccopied, 1)
                for b in range(B):
                    at = (b // PER) * BANK + (b % PER) * N
                    nc.tensor.transpose(g.ps[:, at:at + N], xin[:, b, :], g.ident[0:N, 0:N]).then_inc(turned, 1)

            @block.vector
            def _(dve):
                dve.wait_ge(cturned, 1)
                nc.vector.tensor_copy(g.condT[:, :], g.ps[:, 7 * BANK:7 * BANK + B]).then_inc(ccopied, 1)
                dve.wait_ge(ctanh, 1)
                nc.vector.tensor_scalar(g.csilu[:, :], g.csilu[:, :], 0.5, 0.5, ALU.mult, ALU.add).then_inc(ccopied, 1)
                dve.wait_ge(ccopied, 2)
                nc.vector.tensor_tensor(g.csilu[:, :], g.csilu[:, :], g.condT[:, :], ALU.mult).then_inc(ccopied, 1)
                for c in chunks(dve):
                    dve.wait_ge(turned, PER * (c + 1))
                    nc.vector.tensor_copy(tok(g.xT, c), bank(g, c)).then_inc(copied, 1)

            @block.scalar
            def _(act):
                act.wait_ge(ccopied, 1)
                nc.scalar.activation(g.csilu[:, :], g.condT[:, :], ACT.Tanh, scale=0.5).then_inc(ctanh, 1)



def load_phase(g, loads, mods, clear_stacks=False):
    nc = g.nc
    with ExitStack() as st:
        sem = Sems(g, st)
        loaded, full, ready, stacks_set = sem("weights_loaded"), sem("mod_full"), sem("mod_ready"), sem("stacks_set")
        with nc.Block() as block:
            @block.sync
            def _(sp):
                for dst, src in loads:
                    sp.dma_start(dst, src, allow_slow_non_contiguous=True).then_inc(loaded, 16)
                sp.wait_ge(loaded, 16 * len(loads))

            @block.tensor
            def _(pe):
                pe.wait_ge(loaded, 16 * len(loads))
                for i, (out, w, src, bias, one) in enumerate(mods):
                    nc.tensor.matmul(g.ps[:, i * BANK:i * BANK + B], w, src, start=True, stop=True).then_inc(full, 1)

            @block.gpsimd
            def _(pool):
                if clear_stacks:
                    for s in range(LAG):
                        nc.gpsimd.memset(g.qst[s][:, :, :], 0.0).then_inc(stacks_set, 1)
                    nc.gpsimd.memset(g.kst[1][:, :, 0:2 * CH], 0.0).then_inc(stacks_set, 1)

            @block.vector
            def _(dve):
                if clear_stacks:
                    nc.vector.memset(g.kst[0][SROWS:ROWS, :, 0:LAG * CH], 1.0).then_inc(stacks_set, 1)
                    nc.vector.memset(g.kst[2][:, :, 0:2 * CH], 0.0).then_inc(stacks_set, 1)
                dve.wait_ge(loaded, 16 * len(loads))
                for i, (out, w, src, bias, one) in enumerate(mods):
                    dve.wait_ge(full, i + 1)
                    nc.vector.tensor_scalar(out, g.ps[:, i * BANK:i * BANK + B], bias, 1.0 if one else 0.0,
                                            ALU.add, ALU.add).then_inc(ready, 1)


def l1_mod_phase(g, pairs):
    nc = g.nc
    with ExitStack() as st:
        sem = Sems(g, st)
        done = sem("mod_folded")
        with nc.Block() as block:
            @block.vector
            def _(dve):
                n = 0
                for gamma, beta, ln_g, ln_b in pairs:
                    nc.vector.scalar_tensor_tensor(out=beta, in0=gamma, scalar=ln_b, in1=beta,
                                                   op0=ALU.mult, op1=ALU.add).then_inc(done, 1)
                    n += 1
                    dve.wait_ge(done, n)
                    nc.vector.tensor_scalar(gamma, gamma, ln_g, None, ALU.mult).then_inc(done, 1)
                    n += 1



def project_phase(g, src, xn, eps, mod, projections, residual=None, norm=True, attn=None):
    nc = g.nc
    with ExitStack() as st:
        sem = Sems(g, st)
        sq = st.enter_context(nc.sbuf_tensor(f"sq{g.serial}", [P, T], F32))
        npart = len(projections)
        stacks_set = sem("stacks_set")
        parts = [st.enter_context(nc.sbuf_tensor(f"parts{g.serial}_{i}", [P, 3, T], BF16)) for i in range(npart)]
        A = attention_close_sems(sem) if attn else None
        centered, squared, std_ready, rstd_ready = sem("centered"), sem("squared"), sem("std_ready"), sem("rstd_ready")
        mean_full, var_full, var_read = sem("mean_full"), sem("var_full"), sem("var_read")
        normed, modulated = sem("normed"), sem("modulated")
        full = [sem(f"proj_full{i}") for i in range(npart)]
        f_ready = [sem(f"proj_read{i}") for i in range(npart)]
        high = [sem(f"high{i}") for i in range(npart)]
        rest = [sem(f"rest{i}") for i in range(npart)]
        middle = [sem(f"middle{i}") for i in range(npart)]
        low = [sem(f"low{i}") for i in range(npart)]
        stored = [sem(f"stored{i}") for i in range(npart)]
        x_ready, x_per = A.x(attn) if attn else (None, 1)
        src_tok = lambda c: tok(src, c)
        if norm:
            xin, xin_ready, xin_per = xn, (modulated if mod else normed), (4 if mod else 1)
        else:
            xin, xin_ready, xin_per = src, x_ready, x_per

        with nc.Block() as block:
            @block.tensor
            def _(pe):
                if attn:
                    pe_attention_close(g, pe, attn, A)
                free = A.bank_read if attn else None
                if norm:
                    pe_linear(g, pe, [g.meaner[:, :]], [src_tok], x_ready, x_per, free, mean_full)
                    pe_linear(g, pe, [g.meaner[:, :]], [lambda c: tok(sq, c)], squared, 1, centered, var_full)
                    free = var_read
                for i, (w, bias, dram, scale) in enumerate(projections):
                    pe_linear(g, pe, [w], [lambda c: tok(xin, c)], xin_ready, xin_per, free, full[i])
                    free = f_ready[i]

            @block.vector
            def _(dve):
                if attn:
                    dve_attention_close(g, dve, attn, A)
                if norm:
                    dve_center(g, dve, src, xn, mean_full, centered)
                    dve_variance(g, dve, sq, eps, var_full, var_read)
                    dve_rstd(g, dve, sq, std_ready, rstd_ready)
                    if mod:
                        dve_modulate(g, dve, xn, mod[0], mod[1], normed, modulated)
                for i, (w, bias, dram, scale) in enumerate(projections):
                    for c in chunks(dve):
                        dve.wait_ge(full[i], c + 1)
                        if i:
                            dve.wait_ge(low[i - 1], c + 1)
                        nc.vector.tensor_scalar(tok(sq, c), bank(g, c), bias, scale, ALU.add,
                                                ALU.mult).then_inc(f_ready[i], 1)

            @block.scalar
            def _(act):
                if attn:
                    act_attention_close(g, act, attn, A)
                if norm:
                    act_square(g, act, xn, sq, centered, squared)
                    act_std(g, act, sq, var_read, std_ready)
                for i in range(npart):
                    act_split(g, act, sq, parts[i], f_ready[i], high[i], rest[i], middle[i])

            @block.gpsimd
            def _(pool):
                if attn:
                    pool_attention_close(g, pool, A)
                    pool.wait_ge(A.divided, NCH)
                    for s in range(LAG):
                        nc.gpsimd.memset(g.kst[s][SROWS:ROWS, :, :], 1.0).then_inc(stacks_set, 1)
                    pool.wait_ge(stacks_set, LAG)
                if norm:
                    pool_normalize(g, pool, xn, sq, rstd_ready, normed)
                for i in range(npart):
                    pool_split(g, pool, sq, parts[i], high[i], rest[i], middle[i], low[i])

            @block.sync
            def _(sp):
                for i, (w, bias, dram, scale) in enumerate(projections):
                    sp_parts_out(g, sp, parts[i], dram, low[i], stored[i])



class attention_close_sems:
    def __init__(self, sem):
        self.recip, self.divided, self.o_ready = sem("reciprocal"), sem("divided"), sem("o_ready")
        self.full, self.bank_read, self.gated = sem("out_full"), sem("out_read"), sem("x_gated")

    def x(self, attn):
        return (self.bank_read, 1) if attn["gate"] is None else (self.gated, 4)


def pe_attention_close(g, pe, attn, A):
    pe_linear(g, pe, [attn["w"]], [lambda c: tok(g.oT, c)], A.o_ready, 1, None, A.full)


def dve_attention_close(g, dve, attn, A):
    nc = g.nc
    for c in chunks(dve):
        nc.vector.reciprocal(tok(g.den, c), tok(g.den, c)).then_inc(A.recip, 1)
    if attn["gate"] is None:
        for c in chunks(dve):
            dve.wait_ge(A.full, c + 1)
            nc.vector.scalar_tensor_tensor(out=tok(g.xT, c), in0=bank(g, c), scalar=attn["b"], in1=tok(g.xT, c),
                                           op0=ALU.add, op1=ALU.add).then_inc(A.bank_read, 1)
    else:
        for c in chunks(dve):
            dve.wait_ge(A.bank_read, c + 1)
            for b in batches_of(c):
                nc.vector.scalar_tensor_tensor(out=tok(g.xT, b, N), in0=tok(g.den, b, N),
                                               scalar=attn["gate"][:, bass.ds(b, 1)], in1=tok(g.xT, b, N),
                                               op0=ALU.mult, op1=ALU.add).then_inc(A.gated, 1)


def pool_attention_close(g, pool, A):
    for c in chunks(pool):
        pool.wait_ge(A.recip, c + 1)
        g.nc.gpsimd.tensor_tensor(tok(g.oT, c), tok(g.oT, c), tok(g.den, c), ALU.mult).then_inc(A.divided, 1)


def act_attention_close(g, act, attn, A):
    for c in chunks(act):
        act.wait_ge(A.divided, c + 1)
        g.nc.scalar.activation(tok(g.oT, c), tok(g.oT, c), ACT.Identity, bias=attn["vb"]).then_inc(A.o_ready, 1)
    if attn["gate"] is None:
        return
    for c in chunks(act):
        act.wait_ge(A.full, c + 1)
        g.nc.scalar.activation(tok(g.den, c), bank(g, c), ACT.Identity, bias=attn["b"]).then_inc(A.bank_read, 1)



def mlp_phase(g, attn, eps, mod, w1, b1, w2, b2, gelu, gate):
    nc = g.nc
    with ExitStack() as st:
        sem = Sems(g, st)
        xn = st.enter_context(nc.sbuf_tensor(f"xn{g.serial}", [P, T], F32))
        sq = st.enter_context(nc.sbuf_tensor(f"sq{g.serial}", [P, T], F32))
        h2 = st.enter_context(nc.sbuf_tensor(f"h2_{g.serial}", [P, T], F32))
        hidden = [g.oT, g.den, sq, h2]
        A = attention_close_sems(sem)
        centered, squared, std_ready, rstd_ready = sem("centered"), sem("squared"), sem("std_ready"), sem("rstd_ready")
        mean_full, var_full, var_read = sem("mean_full"), sem("var_full"), sem("var_read")
        normed, modulated = sem("normed"), sem("modulated")
        h_full = [sem(f"hidden_full{m}") for m in range(4)]
        h_ready = [sem(f"hidden_ready{m}") for m in range(4)]
        y_full, y_read, x_done = sem("y_full"), sem("y_read"), sem("x_done")
        with nc.Block() as block:
            @block.tensor
            def _(pe):
                pe_attention_close(g, pe, attn, A)
                pe_linear(g, pe, [g.meaner[:, :]], [lambda c: tok(g.xT, c)], *A.x(attn), A.bank_read, mean_full)
                pe_linear(g, pe, [g.meaner[:, :]], [lambda c: tok(sq, c)], squared, 1, centered, var_full)
                free = var_read
                for m in range(4):
                    pe_linear(g, pe, [w1(m)], [lambda c: tok(xn, c)], modulated, 4, free, h_full[m])
                    free = h_ready[m]
                pe_linear(g, pe, [w2(m) for m in range(4)], [(lambda c, h=h: tok(h, c)) for h in hidden],
                          h_ready[3], 1, None, y_full)

            @block.vector
            def _(dve):
                dve_attention_close(g, dve, attn, A)
                dve_center(g, dve, g.xT, xn, mean_full, centered)
                dve_variance(g, dve, sq, eps, var_full, var_read)
                dve_rstd(g, dve, sq, std_ready, rstd_ready)
                dve_modulate(g, dve, xn, mod[0], mod[1], normed, modulated)
                if gate is None:
                    for c in chunks(dve):
                        dve.wait_ge(y_full, c + 1)
                        nc.vector.scalar_tensor_tensor(out=tok(g.xT, c), in0=bank(g, c), scalar=b2,
                                                       in1=tok(g.xT, c), op0=ALU.add, op1=ALU.add).then_inc(x_done, 1)
                else:
                    for c in chunks(dve):
                        dve.wait_ge(y_read, c + 1)
                        for b in batches_of(c):
                            nc.vector.scalar_tensor_tensor(out=tok(g.xT, b, N), in0=tok(xn, b, N),
                                                           scalar=gate[:, bass.ds(b, 1)], in1=tok(g.xT, b, N),
                                                           op0=ALU.mult, op1=ALU.add).then_inc(x_done, 1)

            @block.gpsimd
            def _(pool):
                pool_attention_close(g, pool, A)
                pool_normalize(g, pool, xn, sq, rstd_ready, normed)

            @block.scalar
            def _(act):
                act_attention_close(g, act, attn, A)
                act_square(g, act, xn, sq, centered, squared)
                act_std(g, act, sq, var_read, std_ready)
                for m in range(4):
                    for c in chunks(act):
                        act.wait_ge(h_full[m], c + 1)
                        if m == 0:
                            act.wait_ge(modulated, B)
                        nc.scalar.activation(tok(hidden[m], c), bank(g, c), gelu,
                                             bias=b1[:, m:m + 1]).then_inc(h_ready[m], 1)
                if gate is not None:
                    for c in chunks(act):
                        act.wait_ge(y_full, c + 1)
                        nc.scalar.activation(tok(xn, c), bank(g, c), ACT.Identity, bias=b2).then_inc(y_read, 1)




def self_attention_phase(g, wv, xn):
    nc, ps = g.nc, g.ps
    GB, G = CH // N, NCH
    H = 2 * GB
    MT = GB * HEADS // 4
    LAST_M, TURN_M = 5, 5
    LD = 16 * SLOTS
    ST_BANK, O_BANKS, M_BANK = 0, (4 * BANK, 7 * BANK), 5 * BANK
    V_BANK = M_BANK + BANK
    with ExitStack() as st:
        sem = Sems(g, st)
        sb = lambda name, shape, dt=F32: st.enter_context(nc.sbuf_tensor(f"{name}_{g.serial}", shape, dt))
        qextra = sb("qextra", [ROWS, PAIRS, 2 * CH], BF16)
        queries = [g.kst[1], g.kst[2], qextra]
        keys = g.kst[0]
        vals = [sb(f"vals{s}", [N, GB, HEADS, VW]) for s in range(LAG)]
        xb = [sb(f"xb{s}", [P, CH]) for s in range(LAG)]
        probs = [sb(f"probs{s}", [P, 8 * N]) for s in range(2)]
        osb = [sb(f"osb{s}", [P, HEADS // 4, GB, N]) for s in range(LAG)]
        maxima = sb("maxima", [N, GB, HEADS])
        negmax = sb("negmax", [HEADS, CH])
        nparts = sb("nparts", [HEADS, 3, CH], BF16)
        slots = lambda name: [sem(f"{name}{s}") for s in range(LAG)]
        set_up, cleared, tokens_ready = sem("set_up"), sem("extra_stack_cleared"), sem("tokens_ready")
        v_full, v_read = sem("values_full"), sem("values_read")
        q_loaded, k_loaded, neg_loaded, o_moved = slots("q_loaded"), slots("k_loaded"), slots("negmax_loaded"), slots("o_moved")
        m_full, m_read, neg_steps = sem("max_full"), sem("max_read"), sem("negmax_steps")
        st_full, exp_done, pv_done, o_read = sem("scores_full"), sem("exp_done"), sem("pv_done"), sem("o_read")
        SET_UP = len(O_BANKS) + LAG
        tiles_by = lambda n: min(MT, -(-MT * (n + 1) // LAST_M))

        def pe_tokens_values(k):
            wait(g.pe, tokens_ready, k.b + 1)
            wait(g.pe, m_read, (MT + 1) * k.b + MT)
            for bb in range(GB):
                ins = nc.tensor.matmul(ps[0:N, V_BANK + P * bb:V_BANK + P * bb + P], xb[k.s][:, N * bb:N * bb + N],
                                       wv, start=True, stop=True)
            ins.then_inc(v_full, 1)

        def pe_max(k, t):
            b, s, r = k.b, k.s, k.r
            if t == 0:
                wait(g.pe, k_loaded[s], LD * (r + 1))
                wait(g.pe, q_loaded[s], 2 * LD * (r + 1))
            wait(g.pe, m_read, (MT + 1) * b + max(t - 1, 0))
            if t == 1:
                wait(g.pe, v_read, b)
            bb = t // 4
            for i in range(4):
                h = 4 * (t % 4) + i
                o = M_BANK + BANK * (t % 2) + N * i
                q0, k0 = CH * (h % 2) + N * bb, CH * s + N * bb
                ins = nc.tensor.matmul(ps[0:N, o:o + N], queries[s][0:SROWS, h // 2, q0:q0 + N],
                                       keys[0:SROWS, h // 2, k0:k0 + N], start=True, stop=True)
            ins.then_inc(m_full, 1)

        def pe_turn_max(k):
            wait(g.pe, m_read, (MT + 1) * k.b + MT)
            for bb in range(GB):
                ins = nc.tensor.transpose(ps[0:HEADS, M_BANK + N * bb:M_BANK + N * bb + N], maxima[:, bb, :], g.ident[0:N, 0:N])
            ins.then_inc(m_full, 1)

        def pe_scores(k, n):
            b, s, r = k.b, k.s, k.r
            bb, hf = n // 2, n % 2
            if n == 0:
                wait(g.pe, neg_loaded[s], 16 * MROWS * (r + 1))
            else:
                wait(g.pe, exp_done, H * b + n - 1)
            k0 = CH * s + N * bb
            for jj in range(4):
                o = ST_BANK + (2 * hf + jj // 2) * BANK + 2 * N * (jj % 2)
                both = queries[s][0:ROWS, 4 * hf + jj, 0:2 * CH].rearrange("p (e n) -> p e n", e=2)[:, :, N * bb:N * bb + N]
                ins = nc.tensor.matmul(ps[0:N, o:o + 2 * N].rearrange("p (e n) -> p e n", e=2),
                                       keys[0:ROWS, 4 * hf + jj, k0:k0 + N], both, start=True, stop=True)
            ins.then_inc(st_full, 1)

        def pe_values(k, n):
            b, s, r = k.b, k.s, k.r
            bb, hf = n // 2, n % 2
            if hf == 0:
                wait(g.pe, o_read, GB * b + bb - 1)
            if n == 0:
                wait(g.pe, v_read, b + 1)
            wait(g.pe, exp_done, H * b + n + 1)
            for i in range(8):
                h = 8 * hf + i
                q = 32 * (h % 4)
                o = O_BANKS[bb % 2] + N * (h // 4)
                ins = nc.tensor.matmul(ps[q:q + VW, o:o + N], vals[s][:, bb, h, :], probs[hf][0:N, N * i:N * i + N],
                                       start=(hf == 0 and i < 4), stop=True, skip_group_check=True)
            ins.then_inc(pv_done, 1)

        def pe_group(k3, k2=None):
            done = 0
            for n in range(H):
                pe_scores(k3, n)
                if k2 is not None:
                    for t in range(done, tiles_by(n)):
                        pe_max(k2, t)
                    done = tiles_by(n)
                if n:
                    pe_values(k3, n - 1)
                if k2 is not None and n == TURN_M:
                    pe_turn_max(k2)
                    pe_tokens_values(k2)
            pe_values(k3, H - 1)

        def act_values(k):
            wait(g.act, v_full, k.b + 1)
            nc.scalar.activation(vals[k.s][:, :, :, 0:HD],
                                 ps[0:N, V_BANK:V_BANK + GB * P].rearrange("p (b h d) -> p b h d", b=GB, h=HEADS),
                                 ACT.Copy).then_inc(v_read, 1)

        def act_group(k3, k2=None):
            for n in range(H):
                hf = n % 2
                wait(g.act, st_full, H * k3.b + n + 1)
                wait(g.act, pv_done, H * k3.b + max(n - 1, 0))
                src = ps[0:N, (2 * hf) * BANK:(2 * hf + 2) * BANK].rearrange("p (k n) -> p k n", k=2)[:, :, 0:CH]
                nc.scalar.activation(probs[hf][0:N, :].rearrange("p (k n) -> p k n", k=2), src, ACT.Exp).then_inc(exp_done, 1)
                if k2 is not None and n == TURN_M + 1:
                    act_values(k2)

        def dve_max(k, t):
            wait(g.dve, m_full, (MT + 1) * k.b + t + 1)
            at, c = M_BANK + BANK * (t % 2), 4 * (t % 4)
            nc.vector.tensor_reduce(maxima[:, t // 4, c:c + 4], ps[0:N, at:at + CH].rearrange("p (h k) -> p h k", h=4),
                                    AX.X, ALU.max).then_inc(m_read, 1)

        def dve_negmax(k):
            b, dve = k.b, g.dve
            wait(dve, m_full, (MT + 1) * (b + 1))
            wait(dve, neg_steps, 4 * b)
            nc.vector.tensor_scalar(negmax[:, :], ps[0:HEADS, M_BANK:M_BANK + CH], -1.0, None, ALU.mult).then_inc(m_read, 1)
            wait(dve, m_read, (MT + 1) * (b + 1))
            p = k.prev()
            wait(dve, neg_loaded[p.s], 16 * MROWS * (p.r + 1))
            nc.vector.tensor_copy(nparts[:, 0, :], negmax[:, :]).then_inc(neg_steps, 1)
            wait(dve, neg_steps, 4 * b + 1)
            nc.vector.tensor_tensor(negmax[:, :], negmax[:, :], nparts[:, 0, :], ALU.subtract).then_inc(neg_steps, 1)
            wait(dve, neg_steps, 4 * b + 2)
            nc.vector.tensor_copy(nparts[:, 1, :], negmax[:, :]).then_inc(neg_steps, 1)
            wait(dve, neg_steps, 4 * b + 3)
            nc.vector.tensor_tensor(nparts[:, 2, :], negmax[:, :], nparts[:, 1, :], ALU.subtract).then_inc(neg_steps, 1)

        def dve_out(k, bb):
            wait(g.dve, pv_done, H * k.b + 2 * bb + 2)
            o = O_BANKS[bb % 2]
            nc.vector.tensor_copy(osb[k.s][:, :, bb, :], ps[:, o:o + CH].rearrange("p (a n) -> p a n", n=N)).then_inc(o_read, 1)

        def dve_group(k3, k2=None):
            if k3 is None:
                for t in range(MT):
                    dve_max(k2, t)
                dve_negmax(k2)
                return
            done = 0
            for n in range(H):
                if k2 is not None:
                    for t in range(done, tiles_by(n)):
                        dve_max(k2, t)
                    done = tiles_by(n)
                if n % 2 == 0 and n:
                    dve_out(k3, n // 2 - 1)
                if k2 is not None and n == TURN_M:
                    dve_negmax(k2)
            dve_out(k3, GB - 1)

        def pool_tokens(k):
            wait(g.pool, v_full, k.b - LAG + 1)
            nc.gpsimd.tensor_tensor(xb[k.s][:, :], tok(xn, k.b), g.zero[:, 0:1].to_broadcast([P, CH]), ALU.add).then_inc(tokens_ready, 1)

        def sp_stacks(k):
            b, s, r, sp = k.b, k.s, k.r, g.sp
            wait(sp, st_full, H * (b - LAG + 1))
            for slot, part in enumerate(Q_PARTS):
                for e in range(2):
                    src = g.qscr[:, part, bass.ds(b * CH, CH)].rearrange("(j q) n -> q j n", q=16)[8 * e:8 * e + 8]
                    at = 16 * slot + 8 * e
                    sp.dma_start(queries[s][at:at + 8, :, CH * e:CH * e + CH], src).then_inc(q_loaded[s], 16)
            for slot, part in enumerate(K_PARTS):
                src = g.kall[:, part, bass.ds(b * CH, CH)].rearrange("(j q) n -> q j n", q=16)
                sp.dma_start(keys[16 * slot:16 * slot + 16, :, CH * s:CH * s + CH], src).then_inc(k_loaded[s], 16)

        def sp_negmax(k):
            s, sp = k.s, g.sp
            wait(sp, neg_steps, 4 * k.b + 4)
            for e in range(2):
                for part in range(3):
                    at = SROWS + 3 * e + part
                    sp.dma_start(queries[s][at:at + 1, :, CH * e:CH * e + CH], nparts[e:HEADS:2, part, :]).then_inc(neg_loaded[s], 16)

        def sp_out(k):
            b, s, r, sp = k.b, k.s, k.r, g.sp
            wait(sp, o_read, GB * (b + 1))
            sp.dma_start(g.oself[s], osb[s][:, :, :, :].rearrange("p a b n -> p (a b n)")).then_inc(o_moved[s], 16)
            wait(sp, o_moved[s], 144 * r + 16)
            src = g.oself[s].rearrange("(c r) (a n) -> a c r n", r=32, n=CH)
            for a in range(4):
                sp.dma_start(g.oT[32 * a:32 * a + 32, bass.ds(b * CH, CH)], src[a, :, 0:HD, :]).then_inc(o_moved[s], 16)
                sp.dma_start(g.den[32 * a:32 * a + 32, bass.ds(b * CH, CH)],
                             src[a, :, HD:HD + 1, :].to_broadcast([4, HD, CH])).then_inc(o_moved[s], 16)

        def sp_group(k3, k2, k1):
            if k1 is not None:
                sp_stacks(k1)
            if k2 is not None:
                sp_negmax(k2)
            sp_out(k3)

        at = lambda i, off: Batch(i, off, LAG)
        known = lambda b: Batch(0, b, LAG) if b < G else None
        loops = (G - 2) // LAG

        with nc.Block() as block:
            @block.tensor
            def _(pe):
                g.pe = pe
                pe.wait_ge(set_up, SET_UP)
                for t in range(MT):
                    pe_max(known(0), t)
                pe_turn_max(known(0))
                pe_tokens_values(known(0))
                pe_group(known(0), known(1))
                with pe.Fori(0, loops) as i:
                    for u in range(1, LAG + 1):
                        pe_group(at(i, u), at(i, u + 1))
                pe_group(known(G - 1))

            @block.scalar
            def _(act):
                g.act = act
                act.wait_ge(set_up, SET_UP)
                act_values(known(0))
                act_group(known(0), known(1))
                with act.Fori(0, loops) as i:
                    for u in range(1, LAG + 1):
                        act_group(at(i, u), at(i, u + 1))
                act_group(known(G - 1))

            @block.vector
            def _(dve):
                g.dve = dve
                nc.vector.memset(qextra[:, :, :], 0.0).then_inc(cleared, 1)
                for o in O_BANKS:
                    nc.vector.memset(ps[:, o:o + CH], 0.0).then_inc(set_up, 1)
                for s in range(LAG):
                    nc.vector.memset(vals[s][:, :, :, HD:VW], 1.0).then_inc(set_up, 1)
                dve_group(None, known(0))
                dve_group(known(0), known(1))
                with dve.Fori(0, loops) as i:
                    for u in range(1, LAG + 1):
                        dve_group(at(i, u), at(i, u + 1))
                dve_group(known(G - 1))

            @block.gpsimd
            def _(pool):
                g.pool = pool
                for b in range(LAG):
                    pool_tokens(known(b))
                for b in range(LAG, G):
                    pool_tokens(known(b))

            @block.sync
            def _(sp):
                g.sp = sp
                sp_stacks(known(0))
                sp_stacks(known(1))
                sp_negmax(known(0))
                sp.wait_ge(cleared, 1)
                for b in range(G):
                    if b == 1:
                        with sp.Fori(0, loops - 1) as i:
                            for u in range(1, LAG + 1):
                                sp_group(at(i, u), at(i, u + 1), at(i, u + 2))
                    if not 1 <= b <= LAG * (loops - 1):
                        sp_group(known(b), known(b + 1), known(b + 2))
                for s in range(LAG):
                    sp.wait_ge(o_moved[s], 144 * len(range(s, G, LAG)))



def cross_attention_phase(g, wk, kb, wv, normed):
    nc, ps = g.nc, g.ps
    kts = KTS
    H2 = 2 * len(kts)
    widths, starts = [482, 482, 480], [0, 482, 964]
    MT = HEADS * 3
    S1 = 9
    ST_BANK, O_BANK, M_BANK, S1_BANK = 0, 4 * BANK, 5 * BANK, 7 * BANK
    PREP_AT = [1, 2, 3, 4, 5, 6, 9, 11, 13] if normed else [0, 1, 2, 3, 4, 5, 8, 11, 14]
    LAST_M, TURN_M, STD_AT = H2 - 8, H2 - 8, H2 - 3
    with ExitStack() as st:
        sem = Sems(g, st)
        sb = lambda name, shape, dt=F32: st.enter_context(nc.sbuf_tensor(f"{name}_{g.serial}", shape, dt))
        vals = [sb(f"vals{s}", [P, len(kts), HEADS, VW]) for s in range(LAG)]
        probs = [sb(f"probs{s}", [P, 8 * N]) for s in range(2)]
        spare = sb("spare", [1, 2])
        osb = [sb(f"osb{s}", [P, CH]) for s in range(LAG)]
        maxima = sb("maxima", [N, MT])
        rowmax = sb("rowmax", [N, HEADS])
        negmax = sb("negmax", [HEADS, N])
        nparts = sb("nparts", [HEADS, 3, N], BF16)
        ctok = [sb(f"ctok{s}", [P, len(kts), P]) for s in range(LAG)]
        ctxT = sb("ctxT", [P, S])
        kf = sb("kf", [P, S])
        parts = sb("kparts", [P, 3, S], BF16)
        if normed:
            stats = sb("stats", [P, len(kts), 6])
            meanvar = sb("meanvar", [P, len(kts), 2])
            rstd = sb("rstd", [P, len(kts)])
        slots = lambda name: [sem(f"{name}{s}") for s in range(LAG)]
        ctx_loaded, ctx_ready = slots("ctx_loaded"), sem("ctx_ready")
        stats_done, aggregated, rstd_done = sem("stats_done"), sem("aggregated"), sem("rstd_done")
        s1_full, s1_read = sem("prep_full"), sem("prep_read")
        split, parts_ready = sem("split_steps"), sem("parts_ready")
        k_moved = slots("k_moved")
        KM = 16 * (SLOTS + 1)
        qst_loaded, neg_loaded = slots("qstack_loaded"), slots("negmax_loaded")
        m_full, m_read, rowmax_ready, neg_steps = sem("max_full"), sem("max_read"), sem("rowmax_ready"), sem("negmax_steps")
        st_full, exp_done, pv_done = sem("scores_full"), sem("exp_done"), sem("pv_done")
        o_read, o_moved = sem("o_read"), slots("o_moved")
        ones, zeros, ctx_std = sem("ones"), sem("zeros"), sem("ctx_std")
        set_up = 1 + 2 * LAG

        def pe_prep(k, t):
            b, s, r = k.b, k.s, k.r
            if t == 0:
                if normed:
                    wait(g.pe, ctx_ready, 4 * (b + 1))
                else:
                    wait(g.pe, ctx_loaded[s], 32 * (r + 1))
            wait(g.pe, s1_read, S1 * b + t)
            if t < 3:
                for i, kt in enumerate(range(4 * t, 4 * t + 4)):
                    n = kts[kt]
                    ins = nc.tensor.transpose(ps[:, S1_BANK + 128 * i:S1_BANK + 128 * i + n], ctok[s][0:n, kt, :],
                                              g.ident[0:n, 0:n])
            elif t < 6:
                a = 512 * (t - 3)
                w = min(512, S - a)
                ins = nc.tensor.matmul(ps[:, S1_BANK:S1_BANK + w], wk, ctxT[:, a:a + w], start=True, stop=True)
            else:
                for i, kt in enumerate(range(4 * (t - 6), 4 * (t - 6) + 4)):
                    n = kts[kt]
                    ins = nc.tensor.matmul(ps[0:n, S1_BANK + 128 * i:S1_BANK + 128 * i + 128],
                                           ctxT[:, 128 * kt:128 * kt + n], wv, start=True, stop=True)
            ins.then_inc(s1_full, 1)

        def pe_max(k, t):
            b, s, r = k.b, k.s, k.r
            if t == 0:
                wait(g.pe, k_moved[s], KM * (r + 1))
                wait(g.pe, qst_loaded[s], 32 * SLOTS * (r + 1))
            wait(g.pe, m_read, (MT + 1) * b + max(t - 1, 0))
            at = M_BANK + BANK * (t % 2)
            h, a, w = t // 3, starts[t % 3], widths[t % 3]
            nc.tensor.matmul(ps[0:N, at:at + w], g.qst[s][0:SROWS, h // 2, N * (h % 2):N * (h % 2) + N],
                             g.kst[s][0:SROWS, h // 2, a:a + w], start=True, stop=True).then_inc(m_full, 1)

        def pe_turn_max(k):
            b, s, r = k.b, k.s, k.r
            wait(g.pe, rowmax_ready, b + 1)
            nc.tensor.transpose(ps[0:HEADS, M_BANK:M_BANK + N], rowmax[:, :], g.ident[0:N, 0:N]).then_inc(m_full, 1)

        def pe_scores(k, n):
            b, s, r = k.b, k.s, k.r
            kt, hf = n // 2, n % 2
            if n == 0:
                wait(g.pe, neg_loaded[s], 16 * MROWS * (r + 1))
            else:
                wait(g.pe, exp_done, H2 * b + n - 1)
            for jj in range(4):
                o = ST_BANK + (2 * hf + jj // 2) * BANK + 2 * N * (jj % 2)
                ins = nc.tensor.matmul(ps[0:kts[kt], o:o + 2 * N],
                                       g.kst[s][0:ROWS, 4 * hf + jj, 128 * kt:128 * kt + kts[kt]],
                                       g.qst[s][0:ROWS, 4 * hf + jj, :], start=True, stop=True)
            ins.then_inc(st_full, 1)

        def pe_values(k, n, half):
            b, s, r = k.b, k.s, k.r
            kt, hf = n // 2, n % 2
            if n == 0 and half == 0:
                wait(g.pe, o_read, b)
                wait(g.pe, s1_read, S1 * (b + 1))
            if half == 0:
                wait(g.pe, exp_done, H2 * b + n + 1)
            for i in range(4 * half, 4 * half + 4):
                h = 8 * hf + i
                q = 32 * (h % 4)
                ins = nc.tensor.matmul(ps[q:q + VW, O_BANK + N * (h // 4):O_BANK + N * (h // 4) + N],
                                       vals[s][:, kt, h, :], probs[hf][:, N * i:N * i + N],
                                       start=(n == 0 and i < 4), stop=(n == H2 - 1 or (n == H2 - 2)),
                                       skip_group_check=True)
            if half:
                ins.then_inc(pv_done, 1)

        def pe_batch(k3, k2=None, k1=None):
            done = 0
            for n in range(H2):
                upto = min(MT, -(-MT * (n + 1) // LAST_M)) if k2 is not None else 0
                tiles = list(range(done, upto))
                done = max(done, upto)
                pe_scores(k3, n)
                for t in tiles[:1]:
                    pe_max(k2, t)
                if k1 is not None and n in PREP_AT:
                    pe_prep(k1, PREP_AT.index(n))
                for t in tiles[1:2]:
                    pe_max(k2, t)
                if n:
                    pe_values(k3, n - 1, 0)
                for t in tiles[2:]:
                    pe_max(k2, t)
                if n:
                    pe_values(k3, n - 1, 1)
                if k2 is not None and n == TURN_M:
                    pe_turn_max(k2)
            for half in range(2):
                pe_values(k3, H2 - 1, half)

        def act_prep(k, t):
            b, s, r = k.b, k.s, k.r
            act = g.act
            wait(act, s1_full, S1 * b + t + 1)
            if t < 3:
                a = 512 * t
                w = min(512, S - a)
                nc.scalar.activation(ctxT[:, a:a + w], ps[:, S1_BANK:S1_BANK + w], ACT.Copy).then_inc(s1_read, 1)
            elif t < 6:
                if t == 3:
                    wait(act, parts_ready, b)
                a = 512 * (t - 3)
                w = min(512, S - a)
                nc.scalar.activation(kf[:, a:a + w], ps[:, S1_BANK:S1_BANK + w], ACT.Identity, bias=kb).then_inc(s1_read, 1)
            else:
                k0 = 4 * (t - 6)
                if t == 6:
                    wait(act, pv_done, H2 * (b - LAG + 1))
                full = 4 if t < 8 else 3
                ins = nc.scalar.activation(vals[s][:, k0:k0 + full, :, 0:HD],
                                           ps[:, S1_BANK:S1_BANK + 128 * full].rearrange("p (k h d) -> p k h d", k=full, h=HEADS),
                                           ACT.Copy)
                if t == 8:
                    n = kts[-1]
                    ins = nc.scalar.activation(vals[s][0:n, 11, :, 0:HD],
                                               ps[0:n, S1_BANK + 384:S1_BANK + 512].rearrange("p (h d) -> p h d", h=HEADS),
                                               ACT.Copy)
                ins.then_inc(s1_read, 1)

        def act_ctx_std(k):
            b, s, r = k.b, k.s, k.r
            wait(g.act, aggregated, len(kts) * (b + 1))
            nc.scalar.activation(rstd[:, :], meanvar[:, :, 1], ACT.Sqrt, bias=g.eps6[:, 0:1]).then_inc(ctx_std, 1)

        def act_exp(k, n):
            b, s, r = k.b, k.s, k.r
            act = g.act
            kt, hf = n // 2, n % 2
            wait(act, st_full, H2 * b + n + 1)
            wait(act, pv_done, H2 * b + max(n - 1, 0))
            src = ps[0:kts[kt], (2 * hf) * BANK:(2 * hf + 2) * BANK].rearrange("p (k n) -> p k n", k=2)[:, :, 0:CH]
            nc.scalar.activation(probs[hf][0:kts[kt], :].rearrange("p (k n) -> p k n", k=2), src, ACT.Exp).then_inc(exp_done, 1)

        def act_batch(k3, k2=None, k1=None, k0=None):
            for n in range(H2):
                act_exp(k3, n)
                if k0 is not None and normed and n == STD_AT:
                    act_ctx_std(k0)
                if k1 is not None and n in PREP_AT:
                    act_prep(k1, PREP_AT.index(n))

        def dve_stats(k):
            b, s, r = k.b, k.s, k.r
            dve = g.dve
            wait(dve, ctx_loaded[s], 32 * (r + 1))
            wait(dve, ctx_ready, 4 * b)
            for kt, n in enumerate(kts):
                nc.vector.bn_stats(stats[0:n, kt, :], ctok[s][0:n, kt, :]).then_inc(stats_done, 1)
            wait(dve, stats_done, len(kts) * (b + 1))
            nc.vector.memset(spare[0:1, 0:1], 0.0)
            for kt, n in enumerate(kts):
                nc.vector.bn_aggr(meanvar[0:n, kt, :], stats[0:n, kt, :]).then_inc(aggregated, 1)

        def dve_ctx_rstd(k):
            b, s, r = k.b, k.s, k.r
            wait(g.dve, ctx_std, b + 1)
            nc.vector.reciprocal(rstd[:, :], rstd[:, :]).then_inc(rstd_done, 1)

        def dve_max(k, t):
            b, s, r = k.b, k.s, k.r
            dve = g.dve
            wait(dve, m_full, (MT + 1) * b + t + 1)
            at = M_BANK + BANK * (t % 2)
            if t == 0:
                wait(dve, rowmax_ready, b)
            nc.vector.reduce_max(maxima[:, t:t + 1], ps[0:N, at:at + widths[t % 3]], AX.X).then_inc(m_read, 1)

        def dve_rowmax(k):
            b, s, r = k.b, k.s, k.r
            dve = g.dve
            wait(dve, m_read, (MT + 1) * b + MT)
            wait(dve, m_full, (MT + 1) * b)
            nc.vector.tensor_reduce(rowmax[:, :], maxima[:, :].rearrange("p (h k) -> p h k", k=3), AX.X,
                                    ALU.max).then_inc(rowmax_ready, 1)

        def dve_negmax(k):
            b, s, r = k.b, k.s, k.r
            dve = g.dve
            wait(dve, m_full, (MT + 1) * (b + 1))
            wait(dve, neg_steps, 4 * b)
            nc.vector.tensor_scalar(negmax[:, :], ps[0:HEADS, M_BANK:M_BANK + N], -1.0, None, ALU.mult).then_inc(m_read, 1)
            wait(dve, m_read, (MT + 1) * (b + 1))
            p = k.prev()
            wait(dve, neg_loaded[p.s], 16 * MROWS * (p.r + 1))
            nc.vector.tensor_copy(nparts[:, 0, :], negmax[:, :]).then_inc(neg_steps, 1)
            wait(dve, neg_steps, 4 * b + 1)
            nc.vector.tensor_tensor(negmax[:, :], negmax[:, :], nparts[:, 0, :], ALU.subtract).then_inc(neg_steps, 1)
            wait(dve, neg_steps, 4 * b + 2)
            nc.vector.tensor_copy(nparts[:, 1, :], negmax[:, :]).then_inc(neg_steps, 1)
            wait(dve, neg_steps, 4 * b + 3)
            nc.vector.tensor_tensor(nparts[:, 2, :], negmax[:, :], nparts[:, 1, :], ALU.subtract).then_inc(neg_steps, 1)

        def dve_out(k):
            b, s, r = k.b, k.s, k.r
            dve = g.dve
            wait(dve, pv_done, H2 * (b + 1))
            nc.vector.tensor_copy(osb[s][:, :], ps[:, O_BANK:O_BANK + CH]).then_inc(o_read, 1)

        def dve_batch(k3, k2=None, k0=None):
            if k2 is not None:
                for t in range(MT):
                    dve_max(k2, t)
                dve_rowmax(k2)
                dve_negmax(k2)
            if k0 is not None and normed:
                dve_stats(k0)
                dve_ctx_rstd(k0)
            if k3 is not None:
                dve_out(k3)

        def pool_copy(out, src):
            return nc.gpsimd.tensor_tensor(out, src, g.zero[0:src.shape[0], 0:1].to_broadcast(list(src.shape)), ALU.add)

        def pool_norm(k):
            b, s, r = k.b, k.s, k.r
            pool = g.pool
            if normed:
                wait(pool, rstd_done, b + 1)
                last, n = len(kts) - 1, kts[-1]
                for step, (column, op) in enumerate(((meanvar[:, :, 0:1], ALU.subtract), (rstd[:, :].unsqueeze(2), ALU.mult))):
                    if step:
                        wait(pool, ctx_ready, 4 * b + 2)
                    nc.gpsimd.tensor_tensor(ctok[s][:, 0:last, :], ctok[s][:, 0:last, :],
                                            column[:, 0:last, :].to_broadcast([P, last, P]), op).then_inc(ctx_ready, 1)
                    nc.gpsimd.tensor_tensor(ctok[s][0:n, last, :], ctok[s][0:n, last, :],
                                            column[0:n, last, :].to_broadcast([n, P]), op).then_inc(ctx_ready, 1)

        def pool_split_keys(k):
            b, s, r = k.b, k.s, k.r
            pool = g.pool
            wait(pool, s1_read, S1 * b + 6)
            p = k.prev()
            wait(pool, k_moved[p.s], KM * (p.r + 1))
            pool_copy(parts[:, 0, :], kf[:, :]).then_inc(split, 1)
            wait(pool, split, 3 * b + 1)
            nc.gpsimd.tensor_tensor(kf[:, :], kf[:, :], parts[:, 0, :], ALU.subtract).then_inc(split, 1)
            wait(pool, split, 3 * b + 2)
            pool_copy(parts[:, 1, :], kf[:, :]).then_inc(split, 1)
            wait(pool, split, 3 * b + 3)
            nc.gpsimd.tensor_tensor(parts[:, 2, :], kf[:, :], parts[:, 1, :], ALU.subtract).then_inc(parts_ready, 1)

        def sp_load_ctx(k):
            b, s, r = k.b, k.s, k.r
            sp = g.sp
            wait(sp, s1_full, S1 * (b - LAG) + 3)
            full = len(kts) - 1
            sp.dma_start(ctok[s][:, 0:full, :], g.ctx[bass.ds(b, 1), 0:128 * full, :].rearrange("a (k p) c -> p (a k) c", p=P)).then_inc(ctx_loaded[s], 16)
            sp.dma_start(ctok[s][0:kts[-1], full, :], g.ctx[bass.ds(b, 1), 128 * full:S, :].rearrange("a p c -> p (a c)")).then_inc(ctx_loaded[s], 16)

        def sp_stacks(k):
            b, s, r = k.b, k.s, k.r
            sp = g.sp
            wait(sp, st_full, H2 * (b - LAG + 1))
            for slot, part in enumerate(Q_PARTS):
                for e in range(2):
                    src = g.qscr[:, part, bass.ds(b * N, N)].rearrange("(j q) n -> q j n", q=16)[8 * e:8 * e + 8]
                    at = 16 * slot + 8 * e
                    sp.dma_start(g.qst[s][at:at + 8, :, N * e:N * e + N], src).then_inc(qst_loaded[s], 16)
            wait(sp, parts_ready, b + 1)
            sp.dma_start(g.kscr[s], parts[:, :, :]).then_inc(k_moved[s], 16)
            wait(sp, k_moved[s], KM * r + 16)
            for slot, part in enumerate(K_PARTS):
                sp.dma_start(g.kst[s][16 * slot:16 * slot + 16, :, :],
                             g.kscr[s][:, part, :].rearrange("(j q) n -> q j n", q=16)).then_inc(k_moved[s], 16)

        def sp_negmax(k):
            b, s, r = k.b, k.s, k.r
            sp = g.sp
            wait(sp, neg_steps, 4 * b + 4)
            for e in range(2):
                for part in range(3):
                    at = SROWS + 3 * e + part
                    sp.dma_start(g.qst[s][at:at + 1, :, N * e:N * e + N], nparts[e:HEADS:2, part, :]).then_inc(neg_loaded[s], 16)

        def sp_out(k):
            b, s, r = k.b, k.s, k.r
            sp = g.sp
            wait(sp, o_read, b + 1)
            sp.dma_start(g.oscr[s], osb[s][:, :]).then_inc(o_moved[s], 16)
            wait(sp, o_moved[s], 144 * r + 16)
            src = g.oscr[s].rearrange("(c r) (a n) -> a c r n", r=32, n=N)
            for a in range(4):
                sp.dma_start(g.oT[32 * a:32 * a + 32, bass.ds(b * N, N)], src[a, :, 0:HD, :]).then_inc(o_moved[s], 16)
                sp.dma_start(g.den[32 * a:32 * a + 32, bass.ds(b * N, N)],
                             src[a, :, HD:HD + 1, :].to_broadcast([4, HD, N])).then_inc(o_moved[s], 16)

        def sp_batch(k0, k3, k2, k1):
            if k0 is not None:
                sp_load_ctx(k0)
            if k1 is not None:
                sp_stacks(k1)
            if k2 is not None:
                sp_negmax(k2)
            if k3 is not None:
                sp_out(k3)

        at = lambda i, off: Batch(i, off, LAG)
        known = lambda b: Batch(0, b, LAG) if 0 <= b < B else None

        loops = (B - 2) // LAG - 1

        with nc.Block() as block:
            @block.tensor
            def _(pe):
                g.pe = pe
                pe.wait_ge(ones, set_up)
                for b in range(2):
                    for t in range(S1):
                        pe_prep(known(b), t)
                for t in range(MT):
                    pe_max(known(0), t)
                pe_turn_max(known(0))
                pe_batch(known(0), known(1), known(2))
                with pe.Fori(0, loops) as i:
                    for u in range(1, LAG + 1):
                        pe_batch(at(i, u), at(i, u + 1), at(i, u + 2))
                for b in range(LAG * loops + 1, B):
                    pe_batch(known(b), known(b + 1), known(b + 2))

            @block.scalar
            def _(act):
                g.act = act
                act.wait_ge(ones, set_up)
                for b in range(2):
                    if normed:
                        act_ctx_std(known(b))
                    for t in range(S1):
                        act_prep(known(b), t)
                if normed:
                    act_ctx_std(known(2))
                act_batch(known(0), known(1), known(2), known(3))
                with act.Fori(0, loops) as i:
                    for u in range(1, LAG + 1):
                        act_batch(at(i, u), at(i, u + 1), at(i, u + 2), at(i, u + 3))
                for b in range(LAG * loops + 1, B):
                    act_batch(known(b), known(b + 1), known(b + 2), known(b + 3))

            @block.vector
            def _(dve):
                g.dve = dve
                nc.vector.memset(ps[:, O_BANK:O_BANK + CH], 0.0).then_inc(ones, 1)
                for s in range(LAG):
                    nc.vector.memset(vals[s][:, len(kts) - 1, :, :], 0.0).then_inc(zeros, 1)
                    nc.vector.memset(vals[s][:, 0:len(kts) - 1, :, HD:VW], 1.0).then_inc(ones, 1)
                    dve.wait_ge(zeros, s + 1)
                    nc.vector.memset(vals[s][0:kts[-1], len(kts) - 1, :, HD:VW], 1.0).then_inc(ones, 1)
                if normed:
                    nc.vector.memset(meanvar[:, :, :], 1.0).then_inc(ones, 1)
                    dve.wait_ge(ones, set_up + 1)
                    for b in range(2):
                        dve_stats(known(b))
                        dve_ctx_rstd(known(b))
                dve_batch(None, known(0), known(2))
                dve_batch(known(0), known(1), known(3))
                with dve.Fori(0, loops) as i:
                    for u in range(1, LAG + 1):
                        dve_batch(at(i, u), at(i, u + 1), at(i, u + 3))
                for b in range(LAG * loops + 1, B):
                    dve_batch(known(b), known(b + 1), known(b + 3))

            @block.gpsimd
            def _(pool):
                g.pool = pool
                for b in range(2):
                    pool_norm(known(b))
                    pool_split_keys(known(b))
                pool_norm(known(2))
                pool_split_keys(known(2))
                pool_norm(known(3))
                with pool.Fori(0, loops) as i:
                    for u in range(1, LAG + 1):
                        pool_split_keys(at(i, u + 2))
                        pool_norm(at(i, u + 3))
                for b in range(LAG * loops + 3, B):
                    pool_split_keys(known(b))
                    if b + 1 < B:
                        pool_norm(known(b + 1))

            @block.sync
            def _(sp):
                g.sp = sp
                sp_load_ctx(known(0))
                sp_batch(known(1), None, None, known(0))
                sp_batch(known(2), None, known(0), known(1))
                sp_batch(known(3), known(0), known(1), known(2))
                with sp.Fori(0, loops) as i:
                    for u in range(1, LAG + 1):
                        sp_batch(at(i, u + 3), at(i, u), at(i, u + 1), at(i, u + 2))
                for b in range(LAG * loops + 1, B):
                    sp_batch(known(b + 3), known(b), known(b + 1), known(b + 2))
                for s in range(LAG):
                    sp.wait_ge(o_moved[s], 144 * len(range(s, B, LAG)))



def l2_query_phase(g, nx, u, gamma, beta, eps, wq, wkT):
    nc = g.nc
    with ExitStack() as st:
        sem = Sems(g, st)
        sq = st.enter_context(nc.sbuf_tensor(f"sq{g.serial}", [P, T], F32))
        centered, squared, std_ready, rstd_ready = sem("centered"), sem("squared"), sem("std_ready"), sem("rstd_ready")
        mean_full, var_full, var_read = sem("mean_full"), sem("var_full"), sem("var_read")
        normed, affine = sem("normed"), sem("affine")
        q_full, q_read, u_full, u_read = sem("q_full"), sem("q_read"), sem("u_full"), sem("u_read")
        with nc.Block() as block:
            @block.tensor
            def _(pe):
                pe_linear(g, pe, [g.meaner[:, :]], [lambda c: tok(g.xT, c)], None, 1, None, mean_full)
                pe_linear(g, pe, [g.meaner[:, :]], [lambda c: tok(sq, c)], squared, 1, centered, var_full)
                pe_linear(g, pe, [wq], [lambda c: tok(nx, c)], affine, 1, var_read, q_full)
                pe_linear(g, pe, [wkT], [lambda c: tok(sq, c)], q_read, 1, q_read, u_full)

            @block.vector
            def _(dve):
                dve_center(g, dve, g.xT, nx, mean_full, centered)
                dve_variance(g, dve, sq, eps, var_full, var_read)
                dve_rstd(g, dve, sq, std_ready, rstd_ready)
                for c in chunks(dve):
                    dve.wait_ge(normed, c + 1)
                    nc.vector.tensor_scalar(tok(nx, c), tok(nx, c), gamma, beta, ALU.mult, ALU.add).then_inc(affine, 1)

            @block.gpsimd
            def _(pool):
                pool_normalize(g, pool, nx, sq, rstd_ready, normed)

            @block.scalar
            def _(act):
                act_square(g, act, nx, sq, centered, squared)
                act_std(g, act, sq, var_read, std_ready)
                for c in chunks(act):
                    act.wait_ge(q_full, c + 1)
                    nc.scalar.activation(tok(sq, c), bank(g, c), ACT.Copy, scale=float(P) ** -0.5).then_inc(q_read, 1)
                for c in chunks(act):
                    act.wait_ge(u_full, c + 1)
                    nc.scalar.activation(tok(u, c), bank(g, c), ACT.Copy).then_inc(u_read, 1)



def l2_attention_phase(g, u):
    nc, ps = g.nc, g.ps
    kts = KTS
    full = len(kts) - 1
    T_BANK, P_BANK, E_BANK = 3 * BANK, 5 * BANK, 7 * BANK
    with ExitStack() as st:
        sem = Sems(g, st)
        sb = lambda name, shape, dt=F32: st.enter_context(nc.sbuf_tensor(f"{name}_{g.serial}", shape, dt))
        ctok = [sb(f"c{s}", [P, len(kts), P]) for s in range(LAG)]
        ctxT = [sb(f"cT{s}", [P, S]) for s in range(LAG)]
        ub = [sb(f"ub{s}", [P, N]) for s in range(LAG)]
        pq = [sb(f"pq{s}", [N, S]) for s in range(LAG)]
        pT = [sb(f"pT{s}", [P, len(kts), N]) for s in range(LAG)]
        mx, nmx, total, inv = ([sb(f"{n}{s}", [N, 1]) for s in range(LAG)] for n in ("mx", "nmx", "tot", "inv"))
        ctx_loaded, u_ready = [sem(f"ctx_loaded{s}") for s in range(LAG)], sem("u_ready")
        t_full, t_read = sem("turned_full"), sem("turned_read")
        s_full, mx_done, nmx_done, exp_done, inv_done, p_norm = (sem("scores_full"), sem("max_done"), sem("negmax_done"),
                                                                 sem("exp_done"), sem("inverse_done"), sem("normalized"))
        p_full, p_read, e_full, e_read = sem("pturned_full"), sem("pturned_read"), sem("evidence_full"), sem("evidence_read")

        def sp_load(sp, k):
            b, s, r = k.b, k.s, k.r
            wait(sp, e_full, b - LAG + 1)
            sp.dma_start(ctok[s][:, 0:full, :], g.ctx[bass.ds(b, 1), 0:128 * full, :].rearrange("a (k p) c -> p (a k) c", p=P)).then_inc(ctx_loaded[s], 16)
            sp.dma_start(ctok[s][0:kts[-1], full, :], g.ctx[bass.ds(b, 1), 128 * full:S, :].rearrange("a p c -> p (a c)")).then_inc(ctx_loaded[s], 16)

        def pe_scores(pe, k):
            b, s, r = k.b, k.s, k.r
            wait(pe, ctx_loaded[s], 32 * (r + 1))
            for t in range(3):
                wait(pe, t_read, 3 * b + max(t - 1, 0))
                for i, kt in enumerate(range(4 * t, 4 * t + 4)):
                    o = T_BANK + BANK * (t % 2) + 128 * i
                    n = kts[kt]
                    ins = nc.tensor.transpose(ps[:, o:o + n], ctok[s][0:n, kt, :], g.ident[0:n, 0:n])
                ins.then_inc(t_full, 1)
            wait(pe, u_ready, b + 1)
            wait(pe, t_read, 3 * (b + 1))
            wait(pe, exp_done, b)
            for t in range(3):
                a = BANK * t
                w = min(BANK, S - a)
                ins = nc.tensor.matmul(ps[0:N, a:a + w], ub[s][:, :], ctxT[s][:, a:a + w], start=True, stop=True)
            ins.then_inc(s_full, 1)

        def pe_evidence(pe, k):
            b, s, r = k.b, k.s, k.r
            wait(pe, p_norm, b + 1)
            for t in range(3):
                wait(pe, p_read, 3 * b + max(t - 1, 0))
                for i, kt in enumerate(range(4 * t, 4 * t + 4)):
                    o = P_BANK + BANK * (t % 2) + N * i
                    n = kts[kt]
                    ins = nc.tensor.transpose(ps[0:n, o:o + N], pq[s][:, 128 * kt:128 * kt + n], g.ident[0:N, 0:N])
                ins.then_inc(p_full, 1)
            wait(pe, p_read, 3 * (b + 1))
            wait(pe, e_read, b)
            for kt, n in enumerate(kts):
                ins = nc.tensor.matmul(ps[:, E_BANK:E_BANK + N], ctok[s][0:n, kt, :], pT[s][0:n, kt, :],
                                       start=(kt == 0), stop=(kt == full))
            ins.then_inc(e_full, 1)

        def act_scores(act, k):
            b, s, r = k.b, k.s, k.r
            for t in range(3):
                wait(act, t_full, 3 * b + t + 1)
                a = BANK * t
                w = min(BANK, S - a)
                if t == 0:
                    wait(act, s_full, b)
                nc.scalar.activation(ctxT[s][:, a:a + w], ps[:, T_BANK + BANK * (t % 2):T_BANK + BANK * (t % 2) + w],
                                     ACT.Copy).then_inc(t_read, 1)
            wait(act, nmx_done, b + 1)
            wait(act, p_full, 3 * (b - 1))
            nc.scalar.activation(pq[s][:, :], ps[0:N, 0:S], ACT.Exp, bias=nmx[s][:, :], accum_out=total[s][:, :]).then_inc(exp_done, 1)

        def dve_scores(dve, k):
            b, s, r = k.b, k.s, k.r
            wait(dve, s_full, b + 1)
            nc.vector.reduce_max(mx[s][:, :], ps[0:N, 0:S], AX.X).then_inc(mx_done, 1)
            wait(dve, mx_done, b + 1)
            wait(dve, exp_done, b - 1)
            nc.vector.tensor_scalar(nmx[s][:, :], mx[s][:, :], -1.0, None, ALU.mult).then_inc(nmx_done, 1)

        def dve_normalize_weights(dve, k):
            b, s, r = k.b, k.s, k.r
            wait(dve, exp_done, b + 1)
            nc.vector.reciprocal(inv[s][:, :], total[s][:, :]).then_inc(inv_done, 1)
            wait(dve, inv_done, b + 1)
            nc.vector.tensor_scalar(pq[s][:, :], pq[s][:, :], inv[s][:, 0:1], None, ALU.mult).then_inc(p_norm, 1)

        def dve_evidence(dve, k):
            b, s, r = k.b, k.s, k.r
            for t in range(3):
                wait(dve, p_full, 3 * b + t + 1)
                if t == 0:
                    wait(dve, e_full, b)
                src = ps[:, P_BANK + BANK * (t % 2):P_BANK + BANK * (t % 2) + CH].rearrange("p (k n) -> p k n", n=N)
                if t < 2:
                    ins = nc.vector.tensor_copy(pT[s][:, 4 * t:4 * t + 4, :], src)
                else:
                    nc.vector.tensor_copy(pT[s][:, 4 * t:4 * t + 3, :], src[:, 0:3, :])
                    ins = nc.vector.tensor_copy(pT[s][0:kts[-1], full, :], src[0:kts[-1], 3, :])
                ins.then_inc(p_read, 1)

        def dve_out(dve, k):
            b, s, r = k.b, k.s, k.r
            wait(dve, e_full, b + 1)
            nc.vector.tensor_copy(g.oT[:, bass.ds(b * N, N)], ps[:, E_BANK:E_BANK + N]).then_inc(e_read, 1)

        def pool_query(pool, k):
            b, s, r = k.b, k.s, k.r
            wait(pool, s_full, b - 1)
            nc.gpsimd.tensor_tensor(ub[s][:, :], u[:, bass.ds(b * N, N)], g.zero[:, 0:1].to_broadcast([P, N]), ALU.add).then_inc(u_ready, 1)

        at = lambda i, off: Batch(i, off, LAG)
        known = lambda b: Batch(0, b, LAG)
        loops = (B - 2) // LAG - 1

        with nc.Block() as block:
            @block.sync
            def _(sp):
                for b in range(LAG):
                    sp_load(sp, known(b))
                with sp.Fori(0, loops) as i:
                    for u in range(LAG):
                        sp_load(sp, at(i, u + LAG))
                for b in range(LAG * (loops + 1), B):
                    sp_load(sp, known(b))

            @block.gpsimd
            def _(pool):
                pool_query(pool, known(0))
                pool_query(pool, known(1))
                with pool.Fori(0, loops + 1) as i:
                    for u in range(LAG):
                        pool_query(pool, at(i, u + 2))

            @block.tensor
            def _(pe):
                pe_scores(pe, known(0))
                pe_scores(pe, known(1))
                pe_evidence(pe, known(0))
                pe_scores(pe, known(2))
                with pe.Fori(0, loops) as i:
                    for u in range(1, LAG + 1):
                        pe_evidence(pe, at(i, u))
                        pe_scores(pe, at(i, u + 2))
                for b in range(LAG * loops + 1, B):
                    pe_evidence(pe, known(b))
                    if b + 2 < B:
                        pe_scores(pe, known(b + 2))

            @block.scalar
            def _(act):
                act_scores(act, known(0))
                act_scores(act, known(1))
                act_scores(act, known(2))
                with act.Fori(0, loops) as i:
                    for u in range(1, LAG + 1):
                        act_scores(act, at(i, u + 2))
                for b in range(LAG * loops + 3, B):
                    act_scores(act, known(b))

            @block.vector
            def _(dve):
                def dve_batch(k, k1, k2):
                    dve_evidence(dve, k)
                    if k1 is not None:
                        dve_normalize_weights(dve, k1)
                    dve_out(dve, k)
                    if k2 is not None:
                        dve_scores(dve, k2)

                dve_scores(dve, known(0))
                dve_normalize_weights(dve, known(0))
                dve_scores(dve, known(1))
                dve_batch(known(0), known(1), known(2))
                with dve.Fori(0, loops) as i:
                    for u in range(1, LAG + 1):
                        dve_batch(at(i, u), at(i, u + 1), at(i, u + 2))
                for b in range(LAG * loops + 1, B):
                    dve_batch(known(b), known(b + 1) if b + 1 < B else None, known(b + 2) if b + 2 < B else None)


def l2_experts_phase(g, nx, w):
    nc = g.nc
    E = 3
    with ExitStack() as st:
        sem = Sems(g, st)
        sb = lambda name: st.enter_context(nc.sbuf_tensor(f"{name}_{g.serial}", [P, T], F32))
        probs = [sb(f"router{e}") for e in range(E)]
        top, h0, h1, routed, term = sb("top"), sb("h0"), sb("h1"), sb("routed"), sb("term")
        ev = g.den
        anchor = lambda c: g.condT[:, bass.ds(c * 4, 4)].unsqueeze(2).to_broadcast([P, 4, N])
        combined = [lambda c: tok(nx, c), lambda c: tok(ev, c), anchor]
        ev_full, ev_read = sem("evidence_full"), sem("evidence_read")
        r_full, r_read = [sem(f"logits_full{e}") for e in range(E)], [sem(f"logits_read{e}") for e in range(E)]
        top1, top2, less = sem("top1"), sem("top2"), sem("logits_less_top")
        exped, sum1, sum2, inv, weights = sem("router_exp"), sem("router_sum1"), sem("router_sum2"), sem("router_inv"), sem("router_weights")
        h_full = [[sem(f"hidden_full{e}{r}") for r in range(2)] for e in range(E)]
        h_read = [[sem(f"hidden_read{e}{r}") for r in range(2)] for e in range(E)]
        y_full, y_read, added = ([sem(f"expert_{n}{e}") for e in range(E)] for n in ("full", "read", "added"))
        g1_full, g1_read, g2_full, g2_read = sem("gate1_full"), sem("gate1_read"), sem("gate2_full"), sem("gate2_read")
        o_full, o_read, x_done = sem("delta_full"), sem("delta_read"), sem("x_done")
        with nc.Block() as block:
            @block.tensor
            def _(pe):
                pe_linear(g, pe, [w["wv"]], [lambda c: tok(g.oT, c)], None, 1, None, ev_full)
                free = ev_read
                for e in range(E):
                    pe_linear(g, pe, [w["router"][:, k, e:e + 1].to_broadcast([P, P]) for k in range(3)], combined,
                              ev_read, 1, free, r_full[e])
                    free = r_read[e]
                for e in range(E):
                    for r in range(2):
                        pe_linear(g, pe, [w["w1"][:, e, k, P * r:P * r + P] for k in range(3)], combined,
                                  None, 1, free, h_full[e][r])
                        free = h_read[e][r]
                    pe_linear(g, pe, [w["w2"][:, e, r, :] for r in range(2)], [lambda c: tok(h0, c), lambda c: tok(h1, c)],
                              free, 1, None, y_full[e])
                    free = y_read[e]
                pe_linear(g, pe, [w["g1"][:, k, :] for k in range(3)], combined, None, 1, free, g1_full)
                pe_linear(g, pe, [w["g2"]], [lambda c: tok(h0, c)], g1_read, 1, None, g2_full)
                pe_linear(g, pe, [w["out"]], [lambda c: tok(routed, c)], added[E - 1], 1, g2_read, o_full)

            @block.scalar
            def _(act):
                for e in range(E):
                    for c in chunks(act):
                        act.wait_ge(r_full[e], c + 1)
                        nc.scalar.activation(tok(probs[e], c), bank(g, c), ACT.Identity, bias=w["rb"][:, e:e + 1]).then_inc(r_read[e], 1)
                for c in chunks(act):
                    act.wait_ge(less, E * (c + 1))
                    for e in range(E):
                        nc.scalar.activation(tok(probs[e], c), tok(probs[e], c), ACT.Exp).then_inc(exped, 1)
                for e in range(E):
                    for r, h in enumerate((h0, h1)):
                        for c in chunks(act):
                            act.wait_ge(h_full[e][r], c + 1)
                            if e:
                                act.wait_ge(y_full[e - 1], c + 1)
                            nc.scalar.activation(tok(h, c), bank(g, c), ACT.Silu, bias=w["b1"][:, 2 * e + r:2 * e + r + 1]).then_inc(h_read[e][r], 1)
                for c in chunks(act):
                    act.wait_ge(g1_full, c + 1)
                    nc.scalar.activation(tok(h0, c), bank(g, c), ACT.Silu, bias=w["gb1"]).then_inc(g1_read, 1)
                for c in chunks(act):
                    act.wait_ge(g2_full, c + 1)
                    nc.scalar.activation(tok(h1, c), bank(g, c), ACT.Sigmoid, bias=w["gb2"]).then_inc(g2_read, 1)

            @block.vector
            def _(dve):
                for c in chunks(dve):
                    dve.wait_ge(ev_full, c + 1)
                    nc.vector.tensor_copy(tok(ev, c), bank(g, c)).then_inc(ev_read, 1)
                for c in chunks(dve):
                    dve.wait_ge(r_read[1], c + 1)
                    nc.vector.tensor_tensor(tok(top, c), tok(probs[0], c), tok(probs[1], c), ALU.max).then_inc(top1, 1)
                for c in chunks(dve):
                    dve.wait_ge(r_read[2], c + 1)
                    dve.wait_ge(top1, c + 1)
                    nc.vector.tensor_tensor(tok(top, c), tok(top, c), tok(probs[2], c), ALU.max).then_inc(top2, 1)
                for c in chunks(dve):
                    dve.wait_ge(top2, c + 1)
                    for e in range(E):
                        nc.vector.tensor_tensor(tok(probs[e], c), tok(probs[e], c), tok(top, c), ALU.subtract).then_inc(less, 1)
                for c in chunks(dve):
                    dve.wait_ge(exped, E * (c + 1))
                    nc.vector.tensor_tensor(tok(top, c), tok(probs[0], c), tok(probs[1], c), ALU.add).then_inc(sum1, 1)
                for c in chunks(dve):
                    dve.wait_ge(sum1, c + 1)
                    nc.vector.tensor_tensor(tok(top, c), tok(top, c), tok(probs[2], c), ALU.add).then_inc(sum2, 1)
                for c in chunks(dve):
                    dve.wait_ge(sum2, c + 1)
                    nc.vector.reciprocal(tok(top, c), tok(top, c)).then_inc(inv, 1)
                for c in chunks(dve):
                    dve.wait_ge(inv, c + 1)
                    for e in range(E):
                        nc.vector.tensor_tensor(tok(probs[e], c), tok(probs[e], c), tok(top, c), ALU.mult).then_inc(weights, 1)
                for e in range(E):
                    for c in chunks(dve):
                        dve.wait_ge(y_full[e], c + 1)
                        dve.wait_ge(weights, E * (c + 1))
                        if e > 1:
                            dve.wait_ge(added[e - 1], c + 1)
                        nc.vector.scalar_tensor_tensor(out=tok(routed if e == 0 else term, c), in0=bank(g, c),
                                                       scalar=w["b2"][:, e:e + 1], in1=tok(probs[e], c),
                                                       op0=ALU.add, op1=ALU.mult).then_inc(y_read[e], 1)
                for c in chunks(dve):
                    dve.wait_ge(o_full, c + 1)
                    dve.wait_ge(added[E - 1], c + 1)
                    nc.vector.scalar_tensor_tensor(out=tok(term, c), in0=bank(g, c), scalar=w["ob"], in1=tok(h1, c),
                                                   op0=ALU.add, op1=ALU.mult).then_inc(o_read, 1)
                for c in chunks(dve):
                    dve.wait_ge(o_read, c + 1)
                    nc.vector.tensor_tensor(tok(g.xT, c), tok(g.xT, c), tok(term, c), ALU.add).then_inc(x_done, 1)

            @block.gpsimd
            def _(pool):
                for e in range(1, E):
                    for c in chunks(pool):
                        pool.wait_ge(y_read[e], c + 1)
                        nc.gpsimd.tensor_tensor(tok(routed, c), tok(routed, c), tok(term, c), ALU.add).then_inc(added[e], 1)


def output_phase(g, out):
    nc = g.nc
    PER = 4
    with ExitStack() as st:
        sem = Sems(g, st)
        xout = st.enter_context(nc.sbuf_tensor("xout", [N, B, P], F32))
        turned, copied, stored = sem("x_turned"), sem("x_copied"), sem("stored")
        with nc.Block() as block:
            @block.tensor
            def _(pe):
                for b in range(B):
                    nc.tensor.transpose(g.ps[0:N, b * P:b * P + P], g.xT[:, b * N:b * N + N], g.ident[:, :]).then_inc(turned, 1)

            @block.vector
            def _(dve):
                for c in range(NCH):
                    dve.wait_ge(turned, PER * (c + 1))
                    nc.vector.tensor_copy(xout[:, PER * c:PER * c + PER, :],
                                          g.ps[0:N, c * BANK:c * BANK + BANK].rearrange("p (b f) -> p b f", f=P)).then_inc(copied, 1)

            @block.sync
            def _(sp):
                for c in range(NCH):
                    sp.wait_ge(copied, c + 1)
                    sp.dma_start(out[PER * c:PER * c + PER, :, :].rearrange("b n p -> n b p"),
                                 xout[:, PER * c:PER * c + PER, :]).then_inc(stored, 16)
                sp.wait_ge(stored, 16 * NCH)


def weight(w):
    return w.rearrange("(k p) m -> p k m", p=P)


def stack_scope(g, stack):
    nc = g.nc
    g.serial += 1
    g.kst = [stack.enter_context(nc.sbuf_tensor(f"kst{s}_{g.serial}", [ROWS, PAIRS, S], BF16)) for s in range(LAG)]
    g.qst = [stack.enter_context(nc.sbuf_tensor(f"qst{s}_{g.serial}", [ROWS, PAIRS, 2 * N], BF16)) for s in range(LAG)]


def transformer_layer(g, a, pre, names, eps, l1):
    nc = g.nc
    with ExitStack() as st:
        g.serial += 1
        sb = lambda name, shape: st.enter_context(nc.sbuf_tensor(f"{name}_{pre}", shape, F32))
        stack_scope(g, st)
        loads = []

        def load(name, src, shape):
            t = sb(name, shape)
            loads.append((t[:], src))
            return t
        mod = sb("mod", [P, 6, B])
        if l1:
            get = lambda n: a[f"L1_xcond_{n}"]
            qkv = [load(f"w{n}", get(f"sa_{n}w"), [P, P])[:, :] for n in "qkv"]
            qkvb = [load(f"b{n}", row(get(f"sa_{n}b")), [P, 1])[:, :] for n in "qkv"]
            wo, bo = load("wo", get("sa_ow"), [P, P]), load("bo", row(get("sa_ob")), [P, 1])
            cqkv = [load(f"cw{n}", get(f"ca_{n}w"), [P, P])[:, :] for n in "qkv"]
            cqkvb = [load(f"cb{n}", row(get(f"ca_{n}b")), [P, 1])[:, :] for n in "qkv"]
            cwo, cbo = load("cwo", get("ca_ow"), [P, P]), load("cbo", row(get("ca_ob")), [P, 1])
            w1, b1 = load("w1", get("ffn_w1"), [P, 4 * P]), load("b1", row(get("ffn_b1")), [P, 4])
            w2, b2 = load("w2", weight(get("ffn_w2")), [P, 4, P]), load("b2", row(get("ffn_b2")), [P, 1])
            aff = [load(f"aff{i}", get(f"aff{i}_w"), [P, 2 * P]) for i in (1, 2)]
            affb = [load(f"affb{i}", row(get(f"aff{i}_b")), [P, 2]) for i in (1, 2)]
            ln = [[load(f"ln{i}{n}", row(get(f"ln{i}_{n}")), [P, 1]) for n in "gb"] for i in (1, 2)]
            mods = [(mod[:, 2 * i + k, :], aff[i][:, P * k:P * k + P], g.condT[:, :], affb[i][:, k:k + 1], False)
                    for i in range(2) for k in range(2)]
            mul1, add1, mul2, add2 = (mod[:, k, :] for k in range(4))
            gate1 = gate2 = None
        else:
            get = lambda n: a[f"{pre}_xcond_{names[n]}"]
            wqkv, bqkv = load("wqkv", get("qkv"), [P, 3 * P]), load("bqkv", row(get("bqkv")), [P, 3])
            qkv = [wqkv[:, P * i:P * i + P] for i in range(3)]
            qkvb = [bqkv[:, i:i + 1] for i in range(3)]
            wo, bo = load("wo", get("o"), [P, P]), load("bo", row(get("bo")), [P, 1])
            wq, bq = load("wq", get("q"), [P, P]), load("bq", row(get("bq")), [P, 1])
            wkv, bkv = load("wkv", get("kv"), [P, 2 * P]), load("bkv", row(get("bkv")), [P, 2])
            cqkv = [wq[:, :], wkv[:, 0:P], wkv[:, P:2 * P]]
            cqkvb = [bq[:, :], bkv[:, 0:1], bkv[:, 1:2]]
            cwo, cbo = load("cwo", get("co"), [P, P]), load("cbo", row(get("bco")), [P, 1])
            w1, b1 = load("w1", get("w1"), [P, 4 * P]), load("b1", row(get("b1")), [P, 4])
            w2, b2 = load("w2", weight(get("w2")), [P, 4, P]), load("b2", row(get("b2")), [P, 1])
            bmod = load("bmod", row(get("bmod")), [P, 6])
            wm = load("wm", get("wmod"), [P, 6 * P])
            mods = [(mod[:, k, :], wm[:, P * k:P * k + P], g.csilu[:, :], bmod[:, k:k + 1], k in (1, 4)) for k in range(6)]
            add1, mul1, gate1, add2, mul2, gate2 = (mod[:, k, :] for k in range(6))
        load_phase(g, loads, mods, clear_stacks=True)
        if l1:
            l1_mod_phase(g, [(mul1, add1, ln[0][0][:, 0:1], ln[0][1][:, 0:1]), (mul2, add2, ln[1][0][:, 0:1], ln[1][1][:, 0:1])])
        self_close = dict(w=wo[:, :], b=bo[:, 0:1], vb=qkvb[2], gate=gate1)
        cross_close = dict(w=cwo[:, :], b=cbo[:, 0:1], vb=cqkvb[2], gate=None)
        with nc.sbuf_tensor(f"xn_{pre}", [P, T], F32) as xn:
            project_phase(g, g.xT, xn, eps, (mul1, add1),
                          [(qkv[0], qkvb[0], g.qscr, SCALE), (qkv[1], qkvb[1], g.kall, 1.0)])
            self_attention_phase(g, qkv[2], xn)
        with nc.sbuf_tensor(f"xn2_{pre}", [P, T], F32) as xn:
            project_phase(g, g.xT, xn, eps, None, [(cqkv[0], cqkvb[0], g.qscr, SCALE)], norm=not l1, attn=self_close)
        cross_attention_phase(g, cqkv[1], cqkvb[1], cqkv[2], normed=(pre == "L0"))
        mlp_phase(g, cross_close, eps, (mul2, add2), lambda m: w1[:, P * m:P * m + P], b1, lambda m: w2[:, m, :],
                  b2[:, 0:1], ACT.Gelu if l1 else ACT.Gelu_apprx_tanh, gate2)


def router_layer(g, a):
    nc = g.nc
    get = lambda n: a[f"L2_xcond_{n}"]
    with ExitStack() as st:
        sb = lambda name, shape: st.enter_context(nc.sbuf_tensor(f"{name}_L2", shape, F32))
        loads = []

        def load(name, src, shape):
            t = sb(name, shape)
            loads.append((t[:], src))
            return t
        gamma, beta = load("gamma", row(get("ln_gamma")), [P, 1]), load("beta", row(get("ln_beta")), [P, 1])
        wq, wk, wv = (load(n, get(n), [P, P]) for n in ("Wq", "Wk", "Wv"))
        wkT = sb("wkT", [P, P])
        router = load("router", weight(get("router_W")), [P, 3, 3])
        rb = load("rb", get("router_b").rearrange("(a e) -> a e", a=1).to_broadcast([P, 3]), [P, 3])
        w1 = load("ew1", get("e_w1").rearrange("e (k p) r -> p (e k) r", p=P), [P, 9, 2 * P])
        b1 = load("eb1", get("e_b1").rearrange("e (r p) -> p (e r)", p=P), [P, 6])
        w2 = load("ew2", get("e_w2").rearrange("e (k p) h -> p (e k) h", p=P), [P, 6, P])
        b2 = load("eb2", get("e_b2").rearrange("e p -> p e"), [P, 3])
        g1, gb1 = load("g1", weight(get("gate_w1")), [P, 3, P]), load("gb1", row(get("gate_b1")), [P, 1])
        g2, gb2 = load("g2", get("gate_w2"), [P, P]), load("gb2", row(get("gate_b2")), [P, 1])
        ow, ob = load("ow", get("out_w"), [P, P]), load("ob", row(get("out_b")), [P, 1])
        load_phase(g, loads, [])
        with ExitStack() as s2:
            sem = Sems(g, s2)
            turned, copied = sem("wk_turned"), sem("wk_copied")
            with nc.Block() as block:
                @block.tensor
                def _(pe):
                    nc.tensor.transpose(g.ps[:, 0:P], wk[:, :], g.ident[:, :]).then_inc(turned, 1)

                @block.vector
                def _(dve):
                    dve.wait_ge(turned, 1)
                    nc.vector.tensor_copy(wkT[:, :], g.ps[:, 0:P]).then_inc(copied, 1)
        nx = sb("nx", [P, T])
        l2_query_phase(g, nx, g.den, gamma[:, 0:1], beta[:, 0:1], 1e-5, wq[:, :], wkT[:, :])
        l2_attention_phase(g, g.den)
        l2_experts_phase(g, nx, dict(wv=wv[:, :], router=router, rb=rb, w1=w1[:].rearrange("p (e k) r -> p e k r", e=3),
                                     b1=b1, w2=w2[:].rearrange("p (e k) r -> p e k r", e=3), b2=b2, g1=g1, gb1=gb1[:, 0:1],
                                     g2=g2[:, :], gb2=gb2[:, 0:1], out=ow[:, :], ob=ob[:, 0:1]))


def program(nc, a, out, layers=(0, 1, 2, 3)):
    g = Ctx()
    g.nc, g.serial = nc, 0
    g.ctx = a["ctx_1024"]
    g.qscr = nc.dram_tensor("q_parts", (P, 3, T), BF16).ap()
    g.kall = nc.dram_tensor("k_parts", (P, 3, T), BF16).ap()
    g.kscr = [nc.dram_tensor(f"ctx_k_parts{s}", (P, 3, S), BF16).ap() for s in range(LAG)]
    g.oself = [nc.dram_tensor(f"o_self_sums{s}", (P, 4 * CH), F32).ap() for s in range(LAG)]
    g.oscr = [nc.dram_tensor(f"o_sums{s}", (P, CH), F32).ap() for s in range(LAG)]
    with ExitStack() as st:
        sb = lambda name, shape: st.enter_context(nc.sbuf_tensor(name, shape, F32))
        g.ps = st.enter_context(nc.psum_tensor("ps", [P, 8 * BANK], F32))
        g.xT, g.oT, g.den = sb("xT", [P, T]), sb("oT", [P, T]), sb("den", [P, T])
        g.ident, g.meaner = sb("ident", [P, P]), sb("meaner", [P, P])
        g.eps6, g.zero = sb("eps6", [P, 1]), sb("zero", [P, 1])
        g.condT, g.csilu = sb("condT", [P, B]), sb("csilu", [P, B])
        setup_phase(g, a["x"], a["cond_1024"])
        n0 = dict(qkv="W_qkv", bqkv="b_qkv", o="W_proj", bo="b_proj", q="W_qc", bq="b_qc", kv="W_kvc", bkv="b_kvc",
                  co="W_cproj", bco="b_cproj", w1="W_mlp1", b1="b_mlp1", w2="W_mlp2", b2="b_mlp2", wmod="W_mod", bmod="b_mod")
        n3 = dict(qkv="qkv_w", bqkv="qkv_b", o="sa_proj_w", bo="sa_proj_b", q="q_w", bq="q_b", kv="kv_w", bkv="kv_b",
                  co="ca_proj_w", bco="ca_proj_b", w1="fc1_w", b1="fc1_b", w2="fc2_w", b2="fc2_b", wmod="adaln_w", bmod="adaln_b")
        if 0 in layers:
            transformer_layer(g, a, "L0", n0, 1e-6, False)
        if 1 in layers:
            transformer_layer(g, a, "L1", {}, 1e-5, True)
        if 2 in layers:
            router_layer(g, a)
        if 3 in layers:
            transformer_layer(g, a, "L3", n3, 1e-6, False)
        output_phase(g, out)



def kernel(**inputs):
    import numpy as _np
    import concourse.bacc as _bacc
    from concourse import mybir as _mybir
    from concourse.bass_utils import run_bass_kernel_spmd as _run

    nc = _bacc.Bacc("TRN2", target_bir_lowering=False, num_devices=1)
    arrays, handles = {}, {}
    for name, value in inputs.items():
        arr = _np.ascontiguousarray(value)
        arrays[f"in_{name}_dram"] = arr
        handles[name] = nc.dram_tensor(f"in_{name}_dram", arr.shape, _mybir.dt.from_np(arr.dtype), kind="ExternalInput").ap()
    out = nc.dram_tensor("out_0_dram", (B, N, P), _mybir.dt.float32, kind="ExternalOutput").ap()
    program(nc, handles, out)
    r = _run(nc, [arrays], core_ids=[0])
    return r.results[0]["out_0_dram"]
```
